# Optimizing a Trainium2 kernel written in Bass

```python
import numpy as np
import jax
import jax.numpy as jnp

def _softmax(x, axis=-1):
    return jax.nn.softmax(x, axis=axis)

def _gelu(x):
    return jax.nn.gelu(x, approximate=True)

def _silu(x):
    return jax.nn.silu(x)

def _sigmoid(x):
    return jax.nn.sigmoid(x)

def _layernorm(x, axis=-1, eps=1e-05):
    m = jnp.mean(x, axis=axis, keepdims=True)
    v = jnp.var(x, axis=axis, keepdims=True)
    return (x - m) / jnp.sqrt(v + eps)

def _scatter_add(tgt, idx, src, axis=0):
    return tgt.at[idx].add(src)

def _segment_sum(src, seg, n):
    return jax.ops.segment_sum(src, seg, n)
kernel_name = 'mk_cond_seq_d1_seqx_r2_ef6715'

def setup_inputs(seed: int=0):
    np.random.seed(seed)
    _w = jnp.asarray

    def _rec_inputs():
        import jax
        import jax.numpy as jnp
        _rk = jax.random.key(seed)
        x = -0.0005207 + 1.001 * jax.random.normal(jax.random.fold_in(_rk, 1), (4, 1024, 512), jnp.float32)
        _lenS = 1024 - jax.random.randint(jax.random.fold_in(_rk, 7), (4,), 0, max(1, 1024 // 4) + 1, jnp.int32)
        _lenS2 = 1024 - jax.random.randint(jax.random.fold_in(_rk, 8), (4,), 0, max(1, 1024 // 4) + 1, jnp.int32)
        cond_2048 = 0.0061147 + 1.02565 * jax.random.normal(jax.random.fold_in(_rk, 11), (4, 1024), jnp.float32)
        cond_1024 = 0.00786388 + 1.0143 * jax.random.normal(jax.random.fold_in(_rk, 12), (4, 512), jnp.float32)
        return (x, cond_2048, cond_1024)
    x, cond_2048, cond_1024 = _rec_inputs()

    def _L0_cond_setup():
        import jax, jax.numpy as jnp
        import numpy as np
        B, S, D, E, N, R = (2, 512, 512, 1024, 16, 64)
        EPS = 1e-05

        def _ln(x, g, b):
            m = jnp.mean(x, -1, keepdims=True)
            v = jnp.mean((x - m) ** 2, -1, keepdims=True)
            return (x - m) * jax.lax.rsqrt(v + EPS) * g + b

        def _ssm(u, Wdbc, Wdt, bdt, Alog, Dp):
            dbc = jnp.einsum('bse,re->bsr', u, Wdbc)
            dlt, Bm, Cm = jnp.split(dbc, [R, R + N], axis=-1)
            delta = jax.nn.softplus(jnp.einsum('bsr,er->bse', dlt, Wdt) + bdt)
            A = -jnp.exp(Alog)
            dA = jnp.exp(delta[..., None] * A)
            dBu = delta[..., None] * Bm[:, :, None, :] * u[..., None]

            def step(h, xs):
                dA_t, dBu_t, C_t = xs
                h = dA_t * h + dBu_t
                y = jnp.einsum('ben,bn->be', h, C_t)
                return (h, y)
            h0 = jnp.zeros((u.shape[0], u.shape[2], N), u.dtype)
            _, ys = jax.lax.scan(step, h0, (dA.swapaxes(0, 1), dBu.swapaxes(0, 1), Cm.swapaxes(0, 1)))
            return ys.swapaxes(0, 1) + u * Dp
        key = jax.random.key(seed)
        ks = jax.random.split(key, 16)
        f = lambda k, sh, s=0.02: jax.random.normal(k, sh, jnp.float32) * s
        Alog = jnp.log(jnp.tile(jnp.arange(1, N + 1, dtype=jnp.float32), (E, 1)))
        return dict(x=f(ks[0], (B, S, D), 1.0), c=f(ks[1], (B, 2 * D), 1.0), w=f(ks[2], (B, D), 1.0), norm1_g=jnp.ones((D,)), norm1_b=jnp.zeros((D,)), norm2_g=jnp.ones((D,)), norm2_b=jnp.zeros((D,)), Wx=f(ks[3], (E, D)), bx=jnp.zeros((E,)), Wz=f(ks[4], (E, D)), bz=jnp.zeros((E,)), Wf=f(ks[5], (D, E)), bf=jnp.zeros((D,)), Wada=f(ks[6], (3 * D, 2 * D)), bada=jnp.zeros((3 * D,)), Wc1=f(ks[7], (E, E)), bc1=jnp.zeros((E,)), Wc2=f(ks[8], (E, E)), bc2=jnp.zeros((E,)), Wdbc1=f(ks[9], (R + 2 * N, E)), Wdt1=f(ks[10], (E, R)), bdt1=jnp.zeros((E,)), Alog1=Alog, Dp1=jnp.ones((E,)), Wdbc2=f(ks[11], (R + 2 * N, E)), Wdt2=f(ks[12], (E, R)), bdt2=jnp.zeros((E,)), Alog2=Alog, Dp2=jnp.ones((E,)))
    _L0_cond_all = _L0_cond_setup()
    _L0_cond_in = {k: v for k, v in _L0_cond_all.items() if k in ('norm1_g', 'norm1_b', 'norm2_g', 'norm2_b', 'Wx', 'bx', 'Wz', 'bz', 'Wf', 'bf', 'Wada', 'bada', 'Wc1', 'bc1', 'Wc2', 'bc2', 'Wdbc1', 'Wdt1', 'bdt1', 'Alog1', 'Dp1', 'Wdbc2', 'Wdt2', 'bdt2', 'Alog2', 'Dp2')}
    del _L0_cond_all
    return {'x': x, 'cond_2048': cond_2048, 'cond_1024': cond_1024, 'L0_cond_norm1_g': _L0_cond_in['norm1_g'], 'L0_cond_norm1_b': _L0_cond_in['norm1_b'], 'L0_cond_norm2_g': _L0_cond_in['norm2_g'], 'L0_cond_norm2_b': _L0_cond_in['norm2_b'], 'L0_cond_Wx': _L0_cond_in['Wx'], 'L0_cond_bx': _L0_cond_in['bx'], 'L0_cond_Wz': _L0_cond_in['Wz'], 'L0_cond_bz': _L0_cond_in['bz'], 'L0_cond_Wf': _L0_cond_in['Wf'], 'L0_cond_bf': _L0_cond_in['bf'], 'L0_cond_Wada': _L0_cond_in['Wada'], 'L0_cond_bada': _L0_cond_in['bada'], 'L0_cond_Wc1': _L0_cond_in['Wc1'], 'L0_cond_bc1': _L0_cond_in['bc1'], 'L0_cond_Wc2': _L0_cond_in['Wc2'], 'L0_cond_bc2': _L0_cond_in['bc2'], 'L0_cond_Wdbc1': _L0_cond_in['Wdbc1'], 'L0_cond_Wdt1': _L0_cond_in['Wdt1'], 'L0_cond_bdt1': _L0_cond_in['bdt1'], 'L0_cond_Alog1': _L0_cond_in['Alog1'], 'L0_cond_Dp1': _L0_cond_in['Dp1'], 'L0_cond_Wdbc2': _L0_cond_in['Wdbc2'], 'L0_cond_Wdt2': _L0_cond_in['Wdt2'], 'L0_cond_bdt2': _L0_cond_in['bdt2'], 'L0_cond_Alog2': _L0_cond_in['Alog2'], 'L0_cond_Dp2': _L0_cond_in['Dp2']}

def reference(x, cond_2048, cond_1024, L0_cond_norm1_g, L0_cond_norm1_b, L0_cond_norm2_g, L0_cond_norm2_b, L0_cond_Wx, L0_cond_bx, L0_cond_Wz, L0_cond_bz, L0_cond_Wf, L0_cond_bf, L0_cond_Wada, L0_cond_bada, L0_cond_Wc1, L0_cond_bc1, L0_cond_Wc2, L0_cond_bc2, L0_cond_Wdbc1, L0_cond_Wdt1, L0_cond_bdt1, L0_cond_Alog1, L0_cond_Dp1, L0_cond_Wdbc2, L0_cond_Wdt2, L0_cond_bdt2, L0_cond_Alog2, L0_cond_Dp2):
    import jax
    import jax.numpy as jnp

    def _L0_cond_ref(x, c, w, norm1_g, norm1_b, norm2_g, norm2_b, Wx, bx, Wz, bz, Wf, bf, Wada, bada, Wc1, bc1, Wc2, bc2, Wdbc1, Wdt1, bdt1, Alog1, Dp1, Wdbc2, Wdt2, bdt2, Alog2, Dp2):
        import jax, jax.numpy as jnp
        import numpy as np
        B, S, D, E, N, R = (2, 512, 512, 1024, 16, 64)
        EPS = 1e-05

        def _ln(x, g, b):
            m = jnp.mean(x, -1, keepdims=True)
            v = jnp.mean((x - m) ** 2, -1, keepdims=True)
            return (x - m) * jax.lax.rsqrt(v + EPS) * g + b

        def _ssm(u, Wdbc, Wdt, bdt, Alog, Dp):
            dbc = jnp.einsum('bse,re->bsr', u, Wdbc)
            dlt, Bm, Cm = jnp.split(dbc, [R, R + N], axis=-1)
            delta = jax.nn.softplus(jnp.einsum('bsr,er->bse', dlt, Wdt) + bdt)
            A = -jnp.exp(Alog)
            dA = jnp.exp(delta[..., None] * A)
            dBu = delta[..., None] * Bm[:, :, None, :] * u[..., None]

            def step(h, xs):
                dA_t, dBu_t, C_t = xs
                h = dA_t * h + dBu_t
                y = jnp.einsum('ben,bn->be', h, C_t)
                return (h, y)
            h0 = jnp.zeros((u.shape[0], u.shape[2], N), u.dtype)
            _, ys = jax.lax.scan(step, h0, (dA.swapaxes(0, 1), dBu.swapaxes(0, 1), Cm.swapaxes(0, 1)))
            return ys.swapaxes(0, 1) + u * Dp
        ada = jax.nn.silu(c) @ Wada.T + bada
        shift, scale, gate = jnp.split(ada, 3, axis=1)
        x_ssm = _ln(x, norm1_g, norm1_b)
        x_ssm = x_ssm * (1.0 + scale[:, None, :]) + shift[:, None, :]
        skip = x_ssm
        x_ssm = _ln(x_ssm, norm2_g, norm2_b)
        mz = jnp.einsum('bsd,ed->bse', x_ssm, Wz) + bz
        mx = jnp.einsum('bsd,ed->bse', x_ssm, Wx) + bx
        act_mx = jax.nn.silu(mx)
        z1 = jnp.einsum('bse,fe->bsf', mz, Wc1) + bc1
        z1 = _ssm(z1, Wdbc1, Wdt1, bdt1, Alog1, Dp1)
        y1 = act_mx * z1
        z2 = jnp.einsum('bse,fe->bsf', mz, Wc2) + bc2
        z2 = jnp.flip(z2, axis=1)
        z2 = _ssm(z2, Wdbc2, Wdt2, bdt2, Alog2, Dp2)
        z2 = jnp.flip(z2, axis=1)
        y2 = act_mx * z2
        out = jnp.einsum('bse,de->bsd', y1 + y2, Wf) + bf + skip
        return x + gate[:, None, :] * out
    x = _L0_cond_ref(x, cond_2048, cond_1024, L0_cond_norm1_g, L0_cond_norm1_b, L0_cond_norm2_g, L0_cond_norm2_b, L0_cond_Wx, L0_cond_bx, L0_cond_Wz, L0_cond_bz, L0_cond_Wf, L0_cond_bf, L0_cond_Wada, L0_cond_bada, L0_cond_Wc1, L0_cond_bc1, L0_cond_Wc2, L0_cond_bc2, L0_cond_Wdbc1, L0_cond_Wdt1, L0_cond_bdt1, L0_cond_Alog1, L0_cond_Dp1, L0_cond_Wdbc2, L0_cond_Wdt2, L0_cond_bdt2, L0_cond_Alog2, L0_cond_Dp2)
    return x

_drawn_inputs = setup_inputs


def setup_inputs(seed=0):
    import zlib

    import numpy as np

    out = dict(_drawn_inputs(seed))
    spreads = {'L0_cond_norm1_g': (1.0, 0.2),
     'L0_cond_norm1_b': (0.0, 0.1),
     'L0_cond_norm2_g': (1.0, 0.2),
     'L0_cond_norm2_b': (0.0, 0.1),
     'L0_cond_bx': (0.0, 0.1),
     'L0_cond_bz': (0.0, 0.1),
     'L0_cond_bf': (0.0, 0.1),
     'L0_cond_bada': (0.0, 0.1),
     'L0_cond_bc1': (0.0, 0.1),
     'L0_cond_bc2': (0.0, 0.1),
     'L0_cond_bdt1': (0.0, 0.1),
     'L0_cond_Dp1': (1.0, 0.2),
     'L0_cond_bdt2': (0.0, 0.1),
     'L0_cond_Dp2': (1.0, 0.2)}
    factors = {}
    for name, (base, spread) in spreads.items():
        noise = np.random.default_rng([zlib.crc32(name.encode()), seed]).standard_normal(out[name].shape)
        drawn = base * np.exp(spread * noise) if base else spread * noise
        out[name] = jnp.asarray(drawn.astype(out[name].dtype))
    for name, factor in factors.items():
        out[name] = (out[name] * factor).astype(out[name].dtype)
    return out
```

```python
import concourse.bass as bass
from concourse import mybir
from contextlib import ExitStack

fp32 = mybir.dt.float32
ALU = mybir.AluOpType
ACT = mybir.ActivationFunctionType

B, S, D, E, N, R = 4, 1024, 512, 1024, 16, 64
P = 128
TC = 512
NC = B * S // TC
DT = D // P
ET = E // P
KE = E // P
TB = TC // P
NG = 4
GR = N // NG
RD = R + 2 * N
SEGS = 4
HALF = [0, 1, 1, 0]
UPB = SEGS * ET
BIG = 30.0
LOW = -40.0
EPS = 1e-5
PA, PBZ, PBD, PDP, PBX, NP_ = 0, N, N + 1, N + 2, N + 3, N + 4


class Count:

    def __init__(self, b, i, per_b, per_i, c):
        self.b, self.i, self.per_b, self.per_i, self.c = b, i, per_b, per_i, c

    def __add__(self, o):
        if isinstance(o, int):
            return Count(self.b, self.i, self.per_b, self.per_i, self.c + o)
        return Count(self.b, self.i, self.per_b + o.per_b, self.per_i + o.per_i, self.c + o.c)

    def __sub__(self, o):
        return self + o * -1

    def __mul__(self, k):
        return Count(self.b, self.i, self.per_b * k, self.per_i * k, self.c * k)

    __rmul__ = __mul__

    def value(self):
        assert self.c >= 0 and self.per_b >= 0 and self.per_i >= 0
        v = self.c
        if self.per_i:
            v = self.i * self.per_i + v
        if self.per_b:
            v = self.b * self.per_b + v
        return v


def value(x):
    return x if isinstance(x, int) else x.value()


def setup_kernel(nc, t, scratch):
    with ExitStack() as ctx:
        def sb(name, shape):
            return ctx.enter_context(nc.sbuf_tensor(name, shape, fp32))

        def sem(name):
            return ctx.enter_context(nc.semaphore(name))

        gate = t["gate"]
        ident = t["ident"]
        xn2 = sb("xn2", [P, NC * TB, D])
        wada = xn2[:, 0:24, :].rearrange("p a d -> p (a d)").rearrange("p (k m) -> p k m", k=KE)
        wz = sb("wz", [P, KE, D])
        gs = sb("gs", [P, B, 2, D])
        wct = sb("wct", [P, 2, KE, P])
        wcz = sb("wcz", [P, 2, D])
        wczt = sb("wczt", [P, 2, D])
        xin = sb("xin", [P, 2, TB, D])
        xsk = sb("xsk", [P, TB, D])
        wdbc = sb("wdbc", [P, 2, KE, RD])
        wproj = sb("wproj", [P, 2, DT, RD])
        xnt = sb("xnt", [P, 2, DT, TC])
        dbo = sb("dbo", [RD, 2, TC])
        bfb = sb("bfb", [P, D])
        par = sb("par", [P, 2, ET, NP_])
        rows = sb("rows", [B, 6, D])
        ct = sb("ct", [P, KE * B])
        cc = sb("cc", [P, KE * B])
        cols = sb("cols", [P, 3, DT])
        bz = sb("bz", [P, KE])
        dbias = sb("dbias", [RD, 2])
        st = sb("st", [P, TB, 6])
        mv = sb("mv", [P, TB, 2])
        ve = sb("ve", [P, TB])
        rs = sb("rs", [P, TB])
        mhalf = sb("mhalf", [P, TB])
        pad = sb("pad", [P, 1])
        shift = sb("shift", [P, D])
        ps = [ctx.enter_context(nc.psum_tensor(f"ps{i}", [P, TC], fp32)) for i in range(8)]

        c_in, wada_in, rows_in, fold_in, cols_in = (sem(n) for n in
                                                    ("c_in", "wada_in", "rows_in", "fold_in", "cols_in"))
        wct_in = [sem(f"wct_in{j}") for j in range(2)]
        id_ready, gs_out, gs_in, par_out = (sem(n) for n in ("id_ready", "gs_out", "gs_in", "par_out"))
        cc_step, silu_ready, ada_mm, row_step, par_ready = (sem(n) for n in (
            "cc_step", "silu_ready", "ada_mm", "row_step", "par_ready"))
        gate_ready, fold_mm, wcz_ready, bcz_ready, wczt_mm, wczt_ready = (sem(n) for n in (
            "gate_ready", "fold_mm", "wcz_ready", "bcz_ready", "wczt_mm", "wczt_ready"))
        proj_ready, bias_ready, bias_mm = (sem(n) for n in ("proj_ready", "bias_ready", "bias_mm"))
        wcz_out = [sem(f"wcz_out{j}") for j in range(2)]
        x_in = [sem(f"x_in{j}") for j in range(2)]
        stats_step, ve_ready, rs_ready, n0_ready, n1_ready, x1_ready, xsk_ready, n2_ready, xsk_out = (
            sem(n) for n in ("stats_step", "ve_ready", "rs_ready", "n0_ready", "n1_ready", "x1_ready",
                             "xsk_ready", "n2_ready", "xsk_out"))
        xnt_mm, xnt_ready, dbc_mm, dbo_ready = (sem(n) for n in (
            "xnt_mm", "xnt_ready", "dbc_mm", "dbo_ready"))
        xnt_out = [sem(f"xnt_out{j}") for j in range(2)]
        dbo_out = [sem(f"dbo_out{j}") for j in range(2)]
        block = ctx.enter_context(nc.Block())
        NF = 2 * ET

        @block.sync
        def _(sp):
            sp.dma_start(ct[:], t["cT"]).then_inc(c_in, 16)
            for n, (src, m) in enumerate((("g1", 0), ("b1", 0), ("bada", 0), ("bada", 1))):
                sp.dma_start(rows[:, n, :], t[src][m * D:(m + 1) * D].partition_broadcast(B)).then_inc(rows_in, 16)
            sp.dma_start(wz[:], t["Wz"]).then_inc(fold_in, 16)
            sp.dma_start(bz[:], t["bz"]).then_inc(fold_in, 16)
            sp.dma_start(wdbc[:], t["wdbcT"]).then_inc(fold_in, 16)
            sp.dma_start(par[:], t["par"]).then_inc(fold_in, 16)
            for n, name in enumerate(("g2", "b2", "bgate")):
                sp.dma_start(cols[:, n, :], t[name]).then_inc(cols_in, 16)
            sp.dma_start(bfb[:], t["bf"].partition_broadcast(P)).then_inc(cols_in, 16)

            def gain_round_trip():
                sp.wait_ge(row_step, 4)
                sp.dma_start(scratch["gs"], rows[:, 4:6, :]).then_inc(gs_out, 16)
                sp.wait_ge(gs_out, 16)
                sp.dma_start(gs[:].rearrange("p b m d -> p (b m d)"),
                             scratch["gs"].rearrange("b m d -> (b m d)").partition_broadcast(P)).then_inc(gs_in, 16)

            for f in range(NF):
                if f >= 2:
                    sp.wait_ge(bias_mm, f - 1)
                sp.dma_start(wct[:, f % 2], t["wcT"][f]).then_inc(wct_in[f % 2], 16)
                if f == 1:
                    gain_round_trip()
                if f >= 3:
                    g = f - 3
                    sp.wait_ge(wczt_ready, g + 1)
                    sp.dma_start(scratch["wz"][g], wczt[:, g % 2, :]).then_inc(wcz_out[g % 2], 16)
            for g in range(NF - 3, NF):
                sp.wait_ge(wczt_ready, g + 1)
                sp.dma_start(scratch["wz"][g], wczt[:, g % 2, :]).then_inc(wcz_out[g % 2], 16)
            sp.wait_ge(par_ready, 2)
            sp.wait_ge(bcz_ready, NF)
            sp.dma_start(scratch["par"].rearrange("f p n -> p f n"),
                         par[:].rearrange("p a e n -> p (a e) n")).then_inc(par_out, 16)
            for c in range(NC):
                for r in ([c, NC] if c == NC - 2 else [c]):
                    if r == c:
                        sp.wait_ge(xnt_ready, DT * (c + 1))
                    sp.dma_start(scratch["xn"][r], xnt[:, c % 2]).then_inc(xnt_out[c % 2], 16)
                for d in range(2):
                    sp.wait_ge(dbo_ready, 2 * c + d + 1)
                    for r in ([c, NC] if c == NC - 2 else [c]):
                        sp.dma_start(scratch["dl"][d, r], dbo[0:R, d, :]).then_inc(dbo_out[d], 16)
                        sp.dma_start(scratch["bc"][d, r], dbo[R:RD, d, :]).then_inc(dbo_out[d], 16)
            sp.wait_ge(par_out, 16)
            for j in range(2):
                sp.wait_ge(wcz_out[j], 16 * NF // 2)
                sp.wait_ge(xnt_out[j], 16 * (NC // 2 + (1 if j == 0 else 0)))
                sp.wait_ge(dbo_out[j], 32 * (NC + 1))

        @block.gpsimd
        def _(pool):
            nc.gpsimd.memset(mhalf[:], -0.5)
            nc.gpsimd.memset(ident[:], 0.0).then_inc(id_ready, 1)
            pool.wait_ge(id_ready, 1)
            nc.gpsimd.affine_select(out=ident[:], in_=ident[:], compare_op=ALU.not_equal, fill=1.0, base=0,
                                    pattern=[[-1, P]], channel_multiplier=1).then_inc(id_ready, 1)
            for k in range(2):
                pool.dma_start(xin[:, k], t["x"][k]).then_inc(x_in[k], 16)
            pool.wait_ge(gs_in, 16)
            pool.wait_ge(cols_in, 64)
            with pool.Fori(0, NC // 2) as b:
                for k in range(2):
                    c = 2 * b + k
                    for half in range(2):
                        pool.wait_ge(ve_ready, 2 * c + half + 1)
                        nc.gpsimd.tensor_tensor(rs[:], ve[:], mhalf[:], ALU.pow).then_inc(rs_ready, 1)
                        if half == 0:
                            for j in range(TB):
                                pool.wait_ge(n1_ready, TB * c + j + 1)
                                nc.gpsimd.tensor_tensor(xin[:, k, j, :], xin[:, k, j, :], shift[:],
                                                        ALU.add).then_inc(x1_ready, 1)
                    pool.wait_ge(x1_ready, TB * c + TB)
                    pool.wait_ge(xsk_out, 16 * c)
                    for j in range(TB):
                        last = nc.gpsimd.tensor_tensor(xsk[:, j, :], xin[:, k, j, :], bfb[:], ALU.add)
                    last.then_inc(xsk_ready, 1)
                    pool.wait_ge(xsk_ready, c + 1)
                    pool.dma_start(scratch["xs"][c], xsk[:]).then_inc(xsk_out, 16)
                    pool.wait_ge(n2_ready, TB * (c + 1))
                    pool.dma_start(xin[:, k], t["x"][c + 2]).then_inc(x_in[k], 16)
            for k in range(2):
                pool.wait_ge(x_in[k], 16 * (NC // 2 + 1))
            pool.wait_ge(xsk_out, 16 * NC)

        @block.scalar
        def _(act):
            act.dma_start(wada, t["wadaT"]).then_inc(wada_in, 16)
            nc.scalar.preload_act_table_set("natural_log_exp_and_others")
            act.wait_ge(cc_step, 1)
            nc.scalar.activation(cc[:], cc[:], ACT.Exp, scale=-1.0).then_inc(cc_step, 1)
            act.wait_ge(cc_step, 2)
            nc.scalar.activation(cc[:], cc[:], ACT.Ln, bias=1.0).then_inc(cc_step, 1)
            act.wait_ge(cc_step, 3)
            nc.scalar.activation(cc[:], cc[:], ACT.Exp, scale=-1.0).then_inc(cc_step, 1)
            act.wait_ge(fold_in, 64)
            nc.scalar.activation(par[:, :, :, PA:PA + N].rearrange("p a e n -> p (a e) n"),
                                 par[:, :, :, PA:PA + N].rearrange("p a e n -> p (a e) n"),
                                 ACT.Exp).then_inc(par_ready, 1)
            for f in range(NF + 1):
                if f < NF:
                    act.wait_ge(fold_mm, f + 1)
                    if f >= 2:
                        act.wait_ge(wczt_mm, f - 1)
                    nc.scalar.activation(wcz[:, f % 2, :], ps[f % 2][:], ACT.Copy).then_inc(wcz_ready, 1)
                    act.wait_ge(bias_mm, f + 1)
                    bcz = par[:, f // ET, f % ET, PBZ:PBZ + 1]
                    nc.scalar.activation(bcz, ps[4][:, f:f + 1], ACT.Identity, bias=bcz).then_inc(bcz_ready, 1)
                if f >= 1:
                    act.wait_ge(wczt_mm, f)
                    if f >= 3:
                        act.wait_ge(wcz_out[(f - 1) % 2], 16 * ((f - 1) // 2))
                    nc.scalar.activation(wczt[:, (f - 1) % 2, :], ps[2 + (f - 1) % 2][:], ACT.Copy).then_inc(wczt_ready, 1)
            act.wait_ge(cols_in, 64)
            for c in range(NC):
                if c >= 2:
                    act.wait_ge(dbc_mm, 2 * (c - 1))
                    act.wait_ge(xnt_out[c % 2], 16 * (c // 2))
                for d in range(DT):
                    act.wait_ge(xnt_mm, DT * c + d + 1)
                    nc.scalar.activation(xnt[:, c % 2, d, :], ps[d][:], ACT.Identity, scale=cols[:, 0, d:d + 1],
                                         bias=cols[:, 1, d:d + 1]).then_inc(xnt_ready, 1)

        @block.vector
        def _(dve):
            dve.wait_ge(c_in, 16)
            nc.vector.tensor_scalar(cc[:], ct[:], LOW, None, ALU.max).then_inc(cc_step, 1)
            dve.wait_ge(cc_step, 4)
            nc.vector.tensor_tensor(ct[:], ct[:], cc[:], ALU.mult).then_inc(silu_ready, 1)
            dve.wait_ge(par_ready, 1)
            nc.vector.tensor_scalar(par[:, :, :, PA:PA + N].rearrange("p a e n -> p (a e) n"),
                                    par[:, :, :, PA:PA + N].rearrange("p a e n -> p (a e) n"),
                                    -1.0, None, ALU.mult).then_inc(par_ready, 1)
            dve.wait_ge(ada_mm, 3)
            dve.wait_ge(rows_in, 64)
            nc.vector.scalar_tensor_tensor(out=rows[:, 3, :], in0=ps[1][0:B, :], scalar=1.0, in1=rows[:, 3, :],
                                           op0=ALU.add, op1=ALU.add).then_inc(row_step, 1)
            nc.vector.tensor_tensor(rows[:, 2, :], ps[0][0:B, :], rows[:, 2, :], ALU.add).then_inc(row_step, 1)
            dve.wait_ge(row_step, 2)
            nc.vector.tensor_tensor(rows[:, 4, :], rows[:, 0, :], rows[:, 3, :], ALU.mult)
            nc.vector.tensor_tensor(rows[:, 1, :], rows[:, 1, :], rows[:, 3, :], ALU.mult).then_inc(row_step, 1)
            dve.wait_ge(row_step, 3)
            nc.vector.tensor_tensor(rows[:, 5, :], rows[:, 1, :], rows[:, 2, :], ALU.add).then_inc(row_step, 1)
            dve.wait_ge(cols_in, 64)
            for d in range(DT):
                nc.vector.tensor_scalar(gate[:, :, d], ps[7][:, d * B:(d + 1) * B], cols[:, 2, d:d + 1], None,
                                        ALU.add).then_inc(gate_ready, 1)
            dve.wait_ge(gs_in, 16)

            def normalise(c, b, k):
                for half in range(2):
                    for j in range(TB):
                        if half == 0 and j == 0:
                            dve.wait_ge(x_in[k], 16 * (b + 1))
                        if half == 1:
                            dve.wait_ge(x1_ready, TB * c + j + 1)
                        nc.vector.bn_stats(st[:, j, :], xin[:, k, j, :]).then_inc(stats_step, 1)
                    dve.wait_ge(stats_step, 16 * c + 8 * half + TB)
                    nc.vector.memset(pad[:], 0.0)
                    for j in range(TB):
                        nc.vector.bn_aggr(mv[:, j, :], st[:, j, :]).then_inc(stats_step, 1)
                    dve.wait_ge(stats_step, 16 * c + 8 * half + 8)
                    nc.vector.tensor_scalar(ve[:], mv[:, :, 1], EPS, None, ALU.add).then_inc(ve_ready, 1)
                    dve.wait_ge(rs_ready, 2 * c + half + 1)
                    for j in range(TB):
                        if half == 0:
                            nc.vector.tensor_scalar(xin[:, k, j, :], xin[:, k, j, :], mv[:, j, 0:1], rs[:, j:j + 1],
                                                    ALU.subtract, ALU.mult).then_inc(n0_ready, 1)
                        else:
                            nc.vector.tensor_scalar(xn2[:, bass.ds(TB * c + j, 1), :], xin[:, k, j, :], mv[:, j, 0:1],
                                                    rs[:, j:j + 1], ALU.subtract, ALU.mult).then_inc(n2_ready, 1)
                    if half == 0:
                        for j in range(TB):
                            dve.wait_ge(n0_ready, TB * c + j + 1)
                            nc.vector.tensor_tensor(xin[:, k, j, :], xin[:, k, j, :], gs[:, bass.ds(b, 1), 0, :],
                                                    ALU.mult).then_inc(n1_ready, 1)

            with dve.Fori(0, NC // 2) as b:
                nc.vector.tensor_copy(shift[:], gs[:, bass.ds(b, 1), 1, :])
                for k in range(2):
                    normalise(2 * b + k, b, k)
            for d in range(2):
                dve.wait_ge(wczt_mm, ET * (d + 1))
                nc.vector.tensor_copy(wproj[:, d].rearrange("p a r -> p (a r)"), ps[5 + d][:, 0:DT * RD]).then_inc(proj_ready, 1)
            nc.vector.tensor_copy(dbias[:], ps[7][0:RD, 32:34]).then_inc(bias_ready, 1)
            dve.wait_ge(bias_ready, 1)
            for c in range(NC):
                for d in range(2):
                    dve.wait_ge(dbc_mm, 2 * c + d + 1)
                    if c >= 1:
                        dve.wait_ge(dbo_out[d], 32 * (c + (1 if c == NC - 1 else 0)))
                    nc.vector.tensor_scalar(dbo[:, d, :], ps[4 + d][0:RD, :], dbias[:, d:d + 1], None,
                                            ALU.add).then_inc(dbo_ready, 1)

        @block.tensor
        def _(pe):
            pe.wait_ge(silu_ready, 1)
            pe.wait_ge(wada_in, 16)
            for d in range(DT):
                for k in range(KE):
                    last = nc.tensor.matmul(ps[7][:, d * B:(d + 1) * B], wada[:, k, 2 * D + d * P:2 * D + (d + 1) * P],
                                            ct[:, k * B:(k + 1) * B], start=(k == 0), stop=(k == KE - 1))
            last.then_inc(ada_mm, 1)
            for m in range(2):
                for k in range(KE):
                    last = nc.tensor.matmul(ps[m][0:B, :], ct[:, k * B:(k + 1) * B], wada[:, k, m * D:(m + 1) * D],
                                            start=(k == 0), stop=(k == KE - 1))
                last.then_inc(ada_mm, 1)
            pe.wait_ge(fold_in, 64)
            pe.wait_ge(id_ready, 2)
            pe.wait_ge(row_step, 2)

            def transposed(f):
                d, e = f // ET, f % ET
                pe.wait_ge(wcz_ready, f + 1)
                if f >= 2:
                    pe.wait_ge(wczt_ready, f - 1)
                for k in range(DT):
                    last = nc.tensor.matmul(ps[2 + f % 2][:, k * P:(k + 1) * P], wcz[:, f % 2, k * P:(k + 1) * P],
                                            ident[:], start=True, stop=True, is_transpose=True)
                for k in range(DT):
                    nc.tensor.matmul(ps[5 + d][:, k * RD:(k + 1) * RD], wcz[:, f % 2, k * P:(k + 1) * P],
                                     wdbc[:, d, e, :], start=(e == 0 and k == 0), stop=(e == ET - 1),
                                     skip_group_check=True)
                pe.wait_ge(bcz_ready, f + 1)
                last = nc.tensor.matmul(ps[7][0:RD, 32 + d:33 + d], wdbc[:, d, e, :], par[:, d, e, PBZ:PBZ + 1],
                                        start=(e == 0), stop=(e == ET - 1), skip_group_check=True)
                last.then_inc(wczt_mm, 1)

            pe.wait_ge(gate_ready, DT)
            for f in range(NF + 1):
                if f < NF:
                    pe.wait_ge(wct_in[f % 2], 16 * (f // 2 + 1))
                    if f >= 2:
                        pe.wait_ge(wcz_ready, f - 1)
                    for k in range(KE):
                        last = nc.tensor.matmul(ps[f % 2][:], wct[:, f % 2, k, :], wz[:, k, :],
                                                start=(k == 0), stop=(k == KE - 1))
                    last.then_inc(fold_mm, 1)
                if f >= 1:
                    transposed(f - 1)
                if f < NF:
                    for k in range(KE):
                        last = nc.tensor.matmul(ps[4][:, f:f + 1], wct[:, f % 2, k, :], bz[:, k:k + 1],
                                                start=(k == 0), stop=(k == KE - 1), skip_group_check=True)
                    last.then_inc(bias_mm, 1)
            pe.wait_ge(wczt_ready, NF)
            for c in range(NC):
                pe.wait_ge(n2_ready, TB * (c + 1))
                for d in range(DT):
                    if c >= 1:
                        pe.wait_ge(xnt_ready, DT * (c - 1) + d + 1)
                    for j in range(TB):
                        last = nc.tensor.matmul(ps[d][:, j * P:(j + 1) * P], xn2[:, TB * c + j, d * P:(d + 1) * P],
                                                ident[:], start=True, stop=True, is_transpose=True)
                    last.then_inc(xnt_mm, 1)
                pe.wait_ge(xnt_ready, DT * (c + 1))
                pe.wait_ge(proj_ready, 2)
                for d in range(2):
                    if c >= 1:
                        pe.wait_ge(dbo_ready, 2 * (c - 1) + d + 1)
                    for k in range(DT):
                        last = nc.tensor.matmul(ps[4 + d][0:RD, :], wproj[:, d, k, :], xnt[:, c % 2, k, :],
                                                start=(k == 0), stop=(k == DT - 1))
                    last.then_inc(dbc_mm, 1)


def ssm_kernel(nc, t, scratch):
    with ExitStack() as ctx:
        def sb(name, shape):
            return ctx.enter_context(nc.sbuf_tensor(name, shape, fp32))

        def sem(name):
            return ctx.enter_context(nc.semaphore(name))

        gate, ident = t["gate"], t["ident"]
        bcb = sb("bcb", [P, 2, GR, NG, TC])
        decay = sb("decay", [P, 2, NG, TC])
        state = sb("state", [P, GR, NG, TC])
        xn = sb("xn", [P, 2, DT, TC])
        dl = sb("dl", [R, 2, TC])
        wzs = sb("wzs", [P, 2, D])
        wdt = sb("wdt", [R, 2, P])
        wx = sb("wx", [P, 2, D])
        wf = sb("wf", [P, 2, D])
        par = sb("upar", [P, 2, NP_])
        u, delta, du, ud = (sb(n, [P, 2, TC]) for n in ("u", "delta", "du", "ud"))
        soft = sb("soft", [P, TC])
        mx, sig, act_mx = (sb(n, [P, TC]) for n in ("mx", "sig", "act_mx"))
        ysum = sb("ysum", [P, TC])
        yout, yfwd, ygate = (sb(n, [P, 2, TC]) for n in ("yout", "yfwd", "ygate"))
        xskip = sb("xskip", [P, TB, D])
        res = sb("res", [P, DT, TC])
        carry = sb("carry", [P, ET * N])
        first_state = sb("first_state", [P, N])
        yps = [ctx.enter_context(nc.psum_tensor(f"yps{j}", [P, TC], fp32)) for j in range(2)]
        zps = ctx.enter_context(nc.psum_tensor("zps", [P, TC], fp32))
        dps = ctx.enter_context(nc.psum_tensor("dps", [P, TC], fp32))
        ops = [ctx.enter_context(nc.psum_tensor(f"ops{d}", [P, TC], fp32)) for d in range(DT)]

        unit_in, tail_in, xn_in, yfwd_in, yout_out = ([sem(f"{n}{j}") for j in range(2)] for n in (
            "unit_in", "tail_in", "xn_in", "yfwd_in", "yout_out"))
        b_in = [sem(f"b_in{g}") for g in range(GR)]
        c_in = [sem(f"c_in{g}") for g in range(GR)]
        xskip_in, res_in, res_out = sem("xskip_in"), sem("res_in"), sem("res_out")
        z_mm, d_mm, mx_mm, group_done, tr_mm, wf_mm, init_mm = (sem(n) for n in (
            "z_mm", "d_mm", "mx_mm", "group_done", "tr_mm", "wf_mm", "init_mm"))
        u_ready, exp_step, soft_ready, ud_ready, decay_ready, mx_ready, sig_step, sig_ready = (sem(n) for n in (
            "u_ready", "exp_step", "soft_ready", "ud_ready", "decay_ready", "mx_ready", "sig_step", "sig_ready"))
        xc_ready, delta_ready, du_ready, scanned, prod_ready, y_read, clamp_ready, act_ready, y_ready, res_ready = (
            sem(n) for n in ("xc_ready", "delta_ready", "du_ready", "scanned", "prod_ready", "y_read",
                             "clamp_ready", "act_ready", "y_ready", "res_ready"))
        carried, saved, dbu_ready = sem("carried"), sem("saved"), sem("dbu_ready")
        block = ctx.enter_context(nc.Block())

        class Unit:
            def __init__(self, b, s, i, n):
                def count(per_b, per_i, c):
                    return Count(b, i, per_b, per_i if n in (1, 2) else 0, c)

                self.b, self.s = count(1, 0, 0), s
                self.first, self.last = n == 0, n == ET - 1
                self.j = n % 2
                self.backward = s >= 2
                tile = count(0, 2, n)
                pair = count(0, 1, n // 2)
                self.tile = tile
                self.q = tile + count(UPB, 0, s * ET)
                self.qs = pair + count(UPB // 2, 0, s * (ET // 2))
                self.v = tile + count(2 * ET, 0, (s - 2) * ET)
                self.vs = pair + count(ET, 0, (s - 2) * (ET // 2))
                self.w = count(2, 0, s - 2)
                self.seg = count(SEGS, 0, s)
                self.stored = pair + count(ET, 0, 0)
                self.next_tile = count(0, 0, 0) if self.last else tile + 1
                self.next_s = (s + 1) % SEGS if self.last else s
                self.next_qs = self.qs + self.j
                self.prev_s = s - 1 if self.first else s
                self.has_prev = not (self.first and s == 0)
                self.prev_tile = count(0, 0, ET - 1) if self.first else tile - 1
                self.prev_qs = self.qs - (1 - self.j)

        def units(eng, unit):
            with eng.Fori(0, B) as b:
                for s in range(SEGS):
                    unit(Unit(b, s, None, 0))
                    with eng.Fori(0, (ET - 2) // 2) as i:
                        unit(Unit(b, s, i, 1))
                        unit(Unit(b, s, i, 2))
                    unit(Unit(b, s, None, ET - 1))

        @block.sync
        def _(sp):
            def row(count):
                v = value(count)
                return v if isinstance(v, int) else sp.snap(v)

            def load_unit(j, tile):
                sp.dma_start(wzs[:, j, :], scratch["wz"][tile]).then_inc(unit_in[j], 16)
                sp.dma_start(wdt[:, j, :], t["wdtT"][tile]).then_inc(unit_in[j], 16)
                sp.dma_start(par[:, j, :], scratch["par"][tile]).then_inc(unit_in[j], 16)

            def load_tokens(chunk, s):
                sp.dma_start(xn[:, s % 2], scratch["xn"][chunk]).then_inc(xn_in[s % 2], 16)
                sp.dma_start(dl[:, s % 2, :], scratch["dl"][s // 2, chunk]).then_inc(xn_in[s % 2], 16)

            def load_row_group(which, chunk, s, g):
                rows = scratch["bc"][s // 2, chunk, N * which + NG * g:N * which + NG * (g + 1), :]
                sp.dma_start(bcb[:, which, g].rearrange("p n t -> p (n t)"),
                             rows.rearrange("n t -> (n t)").partition_broadcast(P)
                             ).then_inc((b_in, c_in)[which][g], 16)

            load_unit(0, 0)
            load_tokens(0, 0)
            for g in range(GR):
                for which in range(2):
                    load_row_group(which, 0, 0, g)

            def unit(x):
                next_row = row(x.next_tile + (x.next_s // 2) * ET)
                if x.backward:
                    tile = row(x.tile)
                if x.first or x.last:
                    chunk, before = row(x.b * 2 + HALF[x.s]), row(x.b * 2 + HALF[x.s - 1])
                    nxt = row(x.b * 2 + (HALF[x.s + 1] if x.s < SEGS - 1 else 2))
                sp.wait_ge(decay_ready, value(GR * x.q))
                load_unit(1 - x.j, next_row)
                if x.backward:
                    if not (x.first and x.s == 2):
                        sp.wait_ge(wf_mm, value(x.v - 1))
                    load_tail(x.j, tile)
                if x.first:
                    sp.wait_ge(z_mm, value(x.q + 2))
                    load_tokens(nxt, (x.s + 1) % SEGS)
                    if x.backward:
                        sp.wait_ge(init_mm, value(x.w))
                        sp.dma_start(xskip[:], scratch["xs"][chunk]).then_inc(xskip_in, 16)
                    if x.s == 3:
                        store_result(before, x.w)
                if x.last:
                    for g in range(GR):
                        for which, used in ((0, dbu_ready), (1, prod_ready)):
                            sp.wait_ge(used, value(GR * x.q + g + 1))
                            load_row_group(which, nxt, (x.s + 1) % SEGS, g)
                    if x.s == 3:
                        store_result(chunk, x.w + 1)

            def load_tail(j, tile):
                sp.dma_start(wx[:, j, :], t["wxT"][tile]).then_inc(tail_in[j], 16)
                sp.dma_start(wf[:, j, :], t["wfT"][tile]).then_inc(tail_in[j], 16)

            def store_result(chunk, segments):
                sp.wait_ge(res_ready, value(DT * segments))
                sp.dma_start(t["out"][chunk], res[:]).then_inc(res_out, 16)

            units(sp, unit)
            sp.wait_ge(res_out, 16 * 2 * B)
            sp.wait_ge(xn_in[0], 32 * (2 * B + 1))
            for g in range(GR):
                sp.wait_ge(b_in[g], 16 * (SEGS * B + 1))
                sp.wait_ge(c_in[g], 16 * (SEGS * B + 1))

        @block.tensor
        def _(pe):
            pe.sem_inc(group_done, GR)

            def prepare_z(j, s, q, qs, b_seg):
                pe.wait_ge(unit_in[j], value(48 * (qs + 1)))
                pe.wait_ge(xn_in[s % 2], value(32 * (b_seg + 1)))
                pe.wait_ge(delta_ready, value(q))
                nc.tensor.matmul(dps[:], wdt[:, j, :], dl[:, s % 2, :], start=True, stop=True).then_inc(d_mm, 1)
                for k in range(DT):
                    last = nc.tensor.matmul(zps[:], wzs[:, j, k * P:(k + 1) * P], xn[:, s % 2, k, :],
                                            start=(k == 0), stop=(k == DT - 1))
                last.then_inc(z_mm, 1)

            def transpose_y(v):
                pe.wait_ge(mx_ready, value(v + 1))
                for k in range(TB):
                    last = nc.tensor.matmul(zps[:, k * P:(k + 1) * P], ysum[:, k * P:(k + 1) * P], ident[:],
                                            start=True, stop=True, is_transpose=True)
                last.then_inc(tr_mm, 1)

            def project(j, v, stop):
                pe.wait_ge(y_ready, value(v + 1))
                for d in range(DT):
                    last = nc.tensor.matmul(ops[d][:], wf[:, j, d * P:(d + 1) * P], ygate[:, j, :],
                                            start=False, stop=stop, skip_group_check=True)
                last.then_inc(wf_mm, 1)

            def unit(x):
                pe.wait_ge(u_ready, value(x.q + 1))
                if x.backward and not (x.first and x.s == 2):
                    pe.wait_ge(mx_ready, value(x.v))
                    pe.wait_ge(y_ready, value(x.v - 1))
                if x.first and x.s == 0:
                    pe.wait_ge(y_ready, value(2 * ET * x.b))
                pairs = x.b * 2 + (x.s // 2) if not x.last else x.b * 2 + ((x.s + 1) // 2)
                prepare_z(1 - x.j, x.next_s, x.q + 1, x.next_qs, pairs)
                for g in range(GR):
                    if g == 0:
                        pe.wait_ge(ud_ready, value(x.q + 1))
                        pe.wait_ge(y_read, value(x.q + 1))
                        for k in range(TB):
                            nc.tensor.matmul(yps[x.j][:, k * P:(k + 1) * P], ud[:, x.j, k * P:(k + 1) * P], ident[:],
                                             start=(k == 0), stop=False, is_transpose=True, skip_group_check=True)
                    pe.wait_ge(prod_ready, value(GR * x.q + g + 1))
                    for n in range(NG):
                        for k in range(TB):
                            last = nc.tensor.matmul(yps[x.j][:, k * P:(k + 1) * P], state[:, g, n, k * P:(k + 1) * P],
                                                    ident[:], start=False, stop=(g == GR - 1 and n == NG - 1),
                                                    is_transpose=True, skip_group_check=True)
                    last.then_inc(group_done, 1)
                    if g == 0 and x.backward:
                        pe.wait_ge(tail_in[x.j], value(32 * (x.vs + 1)))
                        pe.wait_ge(u_ready, value(x.q + 2))
                        for k in range(DT):
                            last = nc.tensor.matmul(zps[:], wx[:, x.j, k * P:(k + 1) * P], xn[:, x.s % 2, k, :],
                                                    start=(k == 0), stop=(k == DT - 1))
                        last.then_inc(mx_mm, 1)
                    if g == 1 and x.prev_s >= 2 and x.has_prev:
                        pe.wait_ge(y_read, value(x.q + 2))
                        transpose_y(x.v)
                    if g == 2 and x.prev_s >= 2 and x.has_prev:
                        project(1 - x.j, x.v - 1, x.first)
                if x.first and x.backward:
                    pe.wait_ge(res_ready, value(DT * x.w))
                    pe.wait_ge(xskip_in, value(16 * (x.w + 1)))
                    for d in range(DT):
                        for k in range(TB):
                            last = nc.tensor.matmul(ops[d][:, k * P:(k + 1) * P], xskip[:, k, d * P:(d + 1) * P],
                                                    ident[:], start=(k == 0), stop=False, is_transpose=True,
                                                    skip_group_check=True)
                    last.then_inc(init_mm, 1)
                if x.last and x.s == 3:
                    pe.wait_ge(y_read, value(x.q + 3))
                    transpose_y(x.v)
                    project(x.j, x.v, True)

            prepare_z(0, 0, 0, 0, 0)
            units(pe, unit)

        @block.scalar
        def _(act):
            def prepare(j, q, qs):
                act.wait_ge(unit_in[j], value(48 * (qs + 1)))
                act.wait_ge(xc_ready, value(q + 1))
                nc.scalar.activation(soft[:], soft[:], ACT.Exp).then_inc(exp_step, 1)
                act.wait_ge(exp_step, value(q + 1))
                nc.scalar.activation(soft[:], soft[:], ACT.Ln, bias=1.0).then_inc(soft_ready, 1)
                act.wait_ge(z_mm, value(q + 1))
                nc.scalar.activation(u[:, j, :], zps[:], ACT.Identity, bias=par[:, j, PBZ:PBZ + 1]).then_inc(u_ready, 1)
                act.wait_ge(u_ready, value(q + 1))
                act.wait_ge(group_done, value(GR * q))
                nc.scalar.activation(ud[:, j, :], u[:, j, :], ACT.Copy, scale=par[:, j, PDP:PDP + 1]).then_inc(ud_ready, 1)

            def unit(x):
                for g in range(GR):
                    if g == 0:
                        act.wait_ge(delta_ready, value(x.q + 1))
                    act.wait_ge(scanned, value(GR * x.q + g + 1))
                    for n in range(NG):
                        m = NG * g + n
                        last = nc.scalar.activation(decay[:, g % 2, n, :], delta[:, x.j, :], ACT.Exp,
                                                    scale=par[:, x.j, PA + m:PA + m + 1])
                    last.then_inc(decay_ready, 1)
                    if g == 1:
                        prepare(1 - x.j, x.q + 1, x.next_qs)
                        if x.backward:
                            act.wait_ge(yout_out[x.j], value((x.stored + (ET // 2 if x.s == 2 else 0) + 1) * 16))
                            act.wait_ge(y_read, value(x.q + 1))
                            act.dma_start(yfwd[:, x.j, :], scratch["y"][HALF[x.s], value(x.tile)]).then_inc(yfwd_in[x.j], 16)
                    if g == 1 and x.last and x.backward:
                        act.wait_ge(res_out, value(16 * x.w))
                        act.dma_start(res[:], t["xT"][value(x.b * 2 + HALF[x.s])]).then_inc(res_in, 16)
                    if g == 2 and x.backward:
                        act.wait_ge(mx_mm, value(x.v + 1))
                        act.wait_ge(act_ready, value(x.v))
                        nc.scalar.activation(mx[:], zps[:], ACT.Identity, bias=par[:, x.j, PBX:PBX + 1]).then_inc(mx_ready, 1)
                if x.has_prev and x.prev_s < 2:
                    act.wait_ge(y_read, value(x.q + 2))
                    act.dma_start(scratch["y"][HALF[x.prev_s], value(x.prev_tile)],
                                  yout[:, 1 - x.j, :]).then_inc(yout_out[1 - x.j], 16)
                if x.backward:
                    act.wait_ge(clamp_ready, value(x.v + 1))
                    nc.scalar.activation(sig[:], sig[:], ACT.Exp, scale=-1.0).then_inc(sig_step, 1)
                    act.wait_ge(sig_step, value(2 * x.v + 1))
                    nc.scalar.activation(sig[:], sig[:], ACT.Ln, bias=1.0).then_inc(sig_step, 1)
                    act.wait_ge(sig_step, value(2 * x.v + 2))
                    nc.scalar.activation(sig[:], sig[:], ACT.Exp, scale=-1.0).then_inc(sig_ready, 1)

            nc.scalar.preload_act_table_set("natural_log_exp_and_others")
            prepare(0, 0, 0)
            units(act, unit)

        @block.gpsimd
        def _(pool):
            def unit(x):
                for g in range(GR):
                    if g == 0:
                        pool.wait_ge(du_ready, value(x.q + 1))
                    pool.wait_ge(b_in[g], value(16 * (x.b * SEGS + x.s + 1)))
                    pool.wait_ge(group_done, value(GR * x.q + g + 1))
                    nc.gpsimd.tensor_tensor(state[:, g], bcb[:, 0, g],
                                            du[:, x.j:x.j + 1, :].broadcast_to([P, NG, TC]),
                                            ALU.mult).then_inc(dbu_ready, 1)

            units(pool, unit)

        @block.vector
        def _(dve):
            dve.sem_inc(scanned, 2)
            dve.sem_inc(y_read, 2)

            def clamp_delta(j, q, qs):
                dve.wait_ge(unit_in[j], value(48 * (qs + 1)))
                dve.wait_ge(d_mm, value(q + 1))
                nc.vector.tensor_scalar(soft[:], dps[:], par[:, j, PBD:PBD + 1], BIG, ALU.add, ALU.min).then_inc(xc_ready, 1)

            def finish_delta(j, q):
                dve.wait_ge(soft_ready, value(q + 1))
                nc.vector.scalar_tensor_tensor(out=delta[:, j, :], in0=dps[:], scalar=par[:, j, PBD:PBD + 1],
                                               in1=soft[:], op0=ALU.add, op1=ALU.max).then_inc(delta_ready, 1)

            def finish_du(j, q):
                dve.wait_ge(delta_ready, value(q + 1))
                dve.wait_ge(u_ready, value(q + 1))
                nc.vector.tensor_tensor(du[:, j, :], delta[:, j, :], u[:, j, :], ALU.mult).then_inc(du_ready, 1)

            def read_y(j, s, q, qs, v, b):
                dve.wait_ge(group_done, value(GR * (q + 2)))
                if s < 2:
                    dve.wait_ge(yout_out[j], value(16 * (qs - b * ET)))
                    nc.vector.tensor_copy(yout[:, j, :], yps[j][:]).then_inc(y_read, 1)
                else:
                    dve.wait_ge(yfwd_in[j], value(16 * (qs - b * ET - ET + 1)))
                    dve.wait_ge(tr_mm, value(v))
                    nc.vector.tensor_tensor(ysum[:], yps[j][:], yfwd[:, j, :], ALU.add).then_inc(y_read, 1)
                    dve.wait_ge(sig_ready, value(v + 1))
                    nc.vector.tensor_tensor(act_mx[:], mx[:], sig[:], ALU.mult).then_inc(act_ready, 1)

            def gate_y(j, v):
                dve.wait_ge(act_ready, value(v + 1))
                dve.wait_ge(tr_mm, value(v + 1))
                nc.vector.tensor_tensor(ygate[:, j, :], zps[:], act_mx[:], ALU.mult).then_inc(y_ready, 1)

            def results(b, w, v):
                dve.wait_ge(wf_mm, value(v))
                dve.wait_ge(res_in, value(16 * (w + 1)))
                for d in range(DT):
                    nc.vector.scalar_tensor_tensor(out=res[:, d, :], in0=ops[d][:], scalar=gate[:, bass.ds(value(b), 1), d],
                                                   in1=res[:, d, :], op0=ALU.mult, op1=ALU.add).then_inc(res_ready, 1)

            def unit(x):
                step = -1 if x.backward else 1
                second = x.s % 2 == 1
                odd = x.b * (2 * ET) + x.tile + (x.s // 2) * ET
                if second:
                    nc.vector.tensor_copy(first_state[:], carry[:, bass.ds(value(x.tile * N), N)]).then_inc(carried, 1)
                    dve.wait_ge(carried, value(odd + 1))
                for g in range(GR):
                    dve.wait_ge(decay_ready, value(GR * x.q + g + 1))
                    dve.wait_ge(dbu_ready, value(GR * x.q + g + 1))
                    for n in range(NG):
                        m = NG * g + n
                        h = state[:, g, n, ::step]
                        last = nc.vector.tensor_tensor_scan(h, decay[:, g % 2, n, ::step], h,
                                                            first_state[:, m:m + 1] if second else 0.0,
                                                            ALU.mult, ALU.add)
                    last.then_inc(scanned, 1)
                    if g == 0:
                        clamp_delta(1 - x.j, x.q + 1, x.next_qs)
                    if g == 1:
                        finish_delta(1 - x.j, x.q + 1)
                    if g == 1 and x.has_prev:
                        read_y(1 - x.j, x.prev_s, x.q - 1, x.prev_qs, x.v - 1 if x.prev_s >= 2 else None, x.b)
                    if g == 1:
                        finish_du(1 - x.j, x.q + 1)
                    if g == 2 and x.backward:
                        dve.wait_ge(mx_ready, value(x.v + 1))
                        nc.vector.tensor_scalar(sig[:], mx[:], LOW, None, ALU.max).then_inc(clamp_ready, 1)
                    dve.wait_ge(scanned, value(GR * x.q + g + 3))
                    if not second:
                        edge = 0 if x.backward else TC - 1
                        nc.vector.tensor_copy(carry[:, bass.ds(value(x.tile * N + NG * g), NG)],
                                              state[:, g, :, edge]).then_inc(saved, 1)
                        dve.wait_ge(saved, value(odd * GR + g + 1))
                    dve.wait_ge(c_in[g], value(16 * (x.b * SEGS + x.s + 1)))
                    nc.vector.tensor_tensor(state[:, g], state[:, g], bcb[:, 1, g], ALU.mult).then_inc(prod_ready, 1)
                    if g == 2 and x.has_prev and x.prev_s >= 2:
                        gate_y(1 - x.j, x.v - 1)
                if x.first and x.s == 3:
                    results(x.b, x.w - 1, x.v)
                if x.last and x.s == 3:
                    read_y(x.j, x.s, x.q, x.qs, x.v, x.b)
                    gate_y(x.j, x.v)
                    results(x.b, x.w, x.v + 1)

            clamp_delta(0, 0, 0)
            finish_delta(0, 0)
            finish_du(0, 0)
            units(dve, unit)


def build(nc, t):
    with ExitStack() as ctx:
        scratch = {
            "gs": nc.dram_tensor("gs_s", (B, 2, D), fp32).ap(),
            "wz": nc.dram_tensor("wz_s", (2 * ET, P, D), fp32).ap(),
            "par": nc.dram_tensor("par_s", (2 * ET, P, NP_), fp32).ap(),
            "xn": nc.dram_tensor("xn_s", (NC + 1, P, DT, TC), fp32).ap(),
            "dl": nc.dram_tensor("dl_s", (2, NC + 1, R, TC), fp32).ap(),
            "bc": nc.dram_tensor("bc_s", (2, NC + 1, 2 * N, TC), fp32).ap(),
            "xs": nc.dram_tensor("xs_s", (NC, P, TB, D), fp32).ap(),
            "y": nc.dram_tensor("y_s", (2, ET, P, TC), fp32).ap(),
        }
        t["gate"] = ctx.enter_context(nc.sbuf_tensor("gate", [P, B, DT], fp32))
        t["ident"] = ctx.enter_context(nc.sbuf_tensor("ident", [P, P], fp32))
        setup_kernel(nc, t, scratch)
        ssm_kernel(nc, t, scratch)


def kernel(**inputs):
    import numpy as np
    import concourse.bacc as bacc
    from concourse.bass_utils import run_bass_kernel_spmd

    a = {k.replace("L0_cond_", ""): np.asarray(v) for k, v in inputs.items()}

    def tiles(m):
        return m.reshape(m.shape[0] // P, P, *m.shape[1:]).swapaxes(0, 1)

    x = a["x"]
    xc = x.reshape(NC, TB, P, D).transpose(0, 2, 1, 3)
    par = np.concatenate([np.concatenate([
        tiles(a[f"Alog{d}"]),
        *(tiles(a[n].reshape(E, 1)) for n in (f"bc{d}", f"bdt{d}", f"Dp{d}", "bx"))], axis=2)[:, None]
        for d in (1, 2)], axis=1)
    arrays = {
        "x": np.concatenate([xc, xc[:2]]),
        "xT": x.reshape(B, 2, TC, DT, P).transpose(0, 1, 4, 3, 2).reshape(NC, P, DT, TC),
        "cT": tiles(a["cond_2048"].T).reshape(P, KE * B),
        "wadaT": tiles(a["Wada"].T),
        "g1": a["norm1_g"], "b1": a["norm1_b"], "bada": a["bada"], "bf": a["bf"],
        "g2": a["norm2_g"].reshape(DT, P).T, "b2": a["norm2_b"].reshape(DT, P).T,
        "bgate": a["bada"][2 * D:].reshape(DT, P).T,
        "Wz": tiles(a["Wz"]), "bz": a["bz"].reshape(KE, P).T,
        "wcT": np.concatenate([a[f"Wc{d}"].reshape(ET, P, KE, P).transpose(0, 3, 2, 1) for d in (1, 2)]),
        "wdbcT": np.stack([tiles(a[f"Wdbc{d}"].T) for d in (1, 2)], axis=1),
        "wdtT": np.concatenate([a[f"Wdt{d}"].reshape(ET, P, R).transpose(0, 2, 1) for d in (1, 2)]),
        "wxT": a["Wx"].reshape(ET, P, DT, P).transpose(0, 3, 2, 1).reshape(ET, P, D),
        "wfT": a["Wf"].T.reshape(ET, P, D),
        "par": par,
    }
    nc = bacc.Bacc("TRN2", target_bir_lowering=False, num_devices=1)
    feed, t = {}, {}
    for name, v in arrays.items():
        v = np.ascontiguousarray(v)
        feed[f"in_{name}"] = v
        t[name] = nc.dram_tensor(f"in_{name}", v.shape, mybir.dt.from_np(v.dtype), kind="ExternalInput").ap()
    t["out"] = nc.dram_tensor("out_t", (NC, P, DT, TC), fp32, kind="ExternalOutput").ap()
    build(nc, t)
    got = run_bass_kernel_spmd(nc, [feed], core_ids=[0])
    return np.ascontiguousarray(got.results[0]["out_t"].transpose(0, 3, 2, 1).reshape(B, S, D))
```

```python
import concourse.bass as bass
from concourse import mybir
from contextlib import ExitStack

fp32 = mybir.dt.float32
ALU = mybir.AluOpType
ACT = mybir.ActivationFunctionType

B, S, D, E, N, R = 4, 1024, 512, 1024, 16, 64
P = 128
TC = 512
NC = B * S // TC
DT = D // P
ET = E // P
KE = E // P
TB = TC // P
NG = 4
GR = N // NG
RD = R + 2 * N
SEGS = 4
HALF = [0, 1, 1, 0]
UPB = SEGS * ET
LOW = -40.0
EPS = 1e-5
PA, PBZ, PBD, PDP, PBX, NP_ = 0, N, N + 1, N + 2, N + 3, N + 4


class Count:

    def __init__(self, b, i, per_b, per_i, c):
        self.b, self.i, self.per_b, self.per_i, self.c = b, i, per_b, per_i, c

    def __add__(self, o):
        if isinstance(o, int):
            return Count(self.b, self.i, self.per_b, self.per_i, self.c + o)
        return Count(self.b, self.i, self.per_b + o.per_b, self.per_i + o.per_i, self.c + o.c)

    def __sub__(self, o):
        return self + o * -1

    def __mul__(self, k):
        return Count(self.b, self.i, self.per_b * k, self.per_i * k, self.c * k)

    __rmul__ = __mul__

    def value(self):
        assert self.c >= 0 and self.per_b >= 0 and self.per_i >= 0
        v = self.c
        if self.per_i:
            v = self.i * self.per_i + v
        if self.per_b:
            v = self.b * self.per_b + v
        return v


def value(x):
    return x if isinstance(x, int) else x.value()


def setup_kernel(nc, t, scratch):
    with ExitStack() as ctx:
        def sb(name, shape):
            return ctx.enter_context(nc.sbuf_tensor(name, shape, fp32))

        def sem(name):
            return ctx.enter_context(nc.semaphore(name))

        gate = t["gate"]
        ident = t["ident"]
        xn2 = sb("xn2", [P, NC * TB, D])
        wada = xn2[:, 0:24, :].rearrange("p a d -> p (a d)").rearrange("p (k m) -> p k m", k=KE)
        wz = sb("wz", [P, KE, D])
        gs = sb("gs", [P, B, 2, D])
        wct = sb("wct", [P, 2, KE, P])
        wcz = sb("wcz", [P, 2, D])
        wczt = sb("wczt", [P, 2, D])
        xin = sb("xin", [P, 2, TB, D])
        xsk = sb("xsk", [P, TB, D])
        wdbc = sb("wdbc", [P, 2, KE, RD])
        wproj = sb("wproj", [P, 2, DT, RD])
        xnt = sb("xnt", [P, 2, DT, TC])
        dbo = sb("dbo", [RD, 2, TC])
        bfb = sb("bfb", [P, D])
        par = sb("par", [P, 2, ET, NP_])
        rows = sb("rows", [B, 6, D])
        ct = sb("ct", [P, KE * B])
        cc = sb("cc", [P, KE * B])
        cols = sb("cols", [P, 3, DT])
        bz = sb("bz", [P, KE])
        dbias = sb("dbias", [RD, 2])
        st = sb("st", [P, TB, 6])
        mv = sb("mv", [P, TB, 2])
        ve = sb("ve", [P, TB])
        rs = sb("rs", [P, TB])
        mhalf = sb("mhalf", [P, TB])
        pad = sb("pad", [P, 1])
        shift = sb("shift", [P, D])
        ps = [ctx.enter_context(nc.psum_tensor(f"ps{i}", [P, TC], fp32)) for i in range(8)]

        c_in, wada_in, rows_in, fold_in, cols_in = (sem(n) for n in
                                                    ("c_in", "wada_in", "rows_in", "fold_in", "cols_in"))
        wct_in = [sem(f"wct_in{j}") for j in range(2)]
        id_ready, gs_out, gs_in, par_out = (sem(n) for n in ("id_ready", "gs_out", "gs_in", "par_out"))
        cc_step, silu_ready, ada_mm, row_step, par_ready = (sem(n) for n in (
            "cc_step", "silu_ready", "ada_mm", "row_step", "par_ready"))
        gate_ready, fold_mm, wcz_ready, bcz_ready, wczt_mm, wczt_ready = (sem(n) for n in (
            "gate_ready", "fold_mm", "wcz_ready", "bcz_ready", "wczt_mm", "wczt_ready"))
        proj_ready, bias_ready, bias_mm = (sem(n) for n in ("proj_ready", "bias_ready", "bias_mm"))
        wcz_out = [sem(f"wcz_out{j}") for j in range(2)]
        x_in = [sem(f"x_in{j}") for j in range(2)]
        stats_step, ve_ready, rs_ready, n0_ready, n1_ready, x1_ready, xsk_ready, n2_ready, xsk_out = (
            sem(n) for n in ("stats_step", "ve_ready", "rs_ready", "n0_ready", "n1_ready", "x1_ready",
                             "xsk_ready", "n2_ready", "xsk_out"))
        xnt_mm, xnt_ready, dbc_mm, dbo_ready = (sem(n) for n in (
            "xnt_mm", "xnt_ready", "dbc_mm", "dbo_ready"))
        xnt_out = [sem(f"xnt_out{j}") for j in range(2)]
        dbo_out = [sem(f"dbo_out{j}") for j in range(2)]
        block = ctx.enter_context(nc.Block())
        NF = 2 * ET

        @block.sync
        def _(sp):
            sp.dma_start(ct[:], t["cT"]).then_inc(c_in, 16)
            for n, (src, m) in enumerate((("g1", 0), ("b1", 0), ("bada", 0), ("bada", 1))):
                sp.dma_start(rows[:, n, :], t[src][m * D:(m + 1) * D].partition_broadcast(B)).then_inc(rows_in, 16)
            sp.dma_start(wz[:], t["Wz"]).then_inc(fold_in, 16)
            sp.dma_start(bz[:], t["bz"]).then_inc(fold_in, 16)
            sp.dma_start(wdbc[:], t["wdbcT"]).then_inc(fold_in, 16)
            sp.dma_start(par[:], t["par"]).then_inc(fold_in, 16)
            for n, name in enumerate(("g2", "b2", "bgate")):
                sp.dma_start(cols[:, n, :], t[name]).then_inc(cols_in, 16)
            sp.dma_start(bfb[:], t["bf"].partition_broadcast(P)).then_inc(cols_in, 16)

            def gain_round_trip():
                sp.wait_ge(row_step, 4)
                sp.dma_start(scratch["gs"], rows[:, 4:6, :]).then_inc(gs_out, 16)
                sp.wait_ge(gs_out, 16)
                sp.dma_start(gs[:].rearrange("p b m d -> p (b m d)"),
                             scratch["gs"].rearrange("b m d -> (b m d)").partition_broadcast(P)).then_inc(gs_in, 16)

            for f in range(NF):
                if f >= 2:
                    sp.wait_ge(bias_mm, f - 1)
                sp.dma_start(wct[:, f % 2], t["wcT"][f]).then_inc(wct_in[f % 2], 16)
                if f == 1:
                    gain_round_trip()
                if f >= 3:
                    g = f - 3
                    sp.wait_ge(wczt_ready, g + 1)
                    sp.dma_start(scratch["wz"][g], wczt[:, g % 2, :]).then_inc(wcz_out[g % 2], 16)
            for g in range(NF - 3, NF):
                sp.wait_ge(wczt_ready, g + 1)
                sp.dma_start(scratch["wz"][g], wczt[:, g % 2, :]).then_inc(wcz_out[g % 2], 16)
            sp.wait_ge(par_ready, 2)
            sp.wait_ge(bcz_ready, NF)
            sp.dma_start(scratch["par"].rearrange("f p n -> p f n"),
                         par[:].rearrange("p a e n -> p (a e) n")).then_inc(par_out, 16)
            for c in range(NC):
                for r in ([c, NC] if c == NC - 2 else [c]):
                    if r == c:
                        sp.wait_ge(xnt_ready, DT * (c + 1))
                    sp.dma_start(scratch["xn"][r], xnt[:, c % 2]).then_inc(xnt_out[c % 2], 16)
                for d in range(2):
                    sp.wait_ge(dbo_ready, 2 * c + d + 1)
                    for r in ([c, NC] if c == NC - 2 else [c]):
                        sp.dma_start(scratch["dl"][d, r], dbo[0:R, d, :]).then_inc(dbo_out[d], 16)
                        sp.dma_start(scratch["bc"][d, r], dbo[R:RD, d, :]).then_inc(dbo_out[d], 16)
            sp.wait_ge(par_out, 16)
            for j in range(2):
                sp.wait_ge(wcz_out[j], 16 * NF // 2)
                sp.wait_ge(xnt_out[j], 16 * (NC // 2 + (1 if j == 0 else 0)))
                sp.wait_ge(dbo_out[j], 32 * (NC + 1))

        @block.gpsimd
        def _(pool):
            nc.gpsimd.memset(mhalf[:], -0.5)
            nc.gpsimd.memset(ident[:], 0.0).then_inc(id_ready, 1)
            pool.wait_ge(id_ready, 1)
            nc.gpsimd.affine_select(out=ident[:], in_=ident[:], compare_op=ALU.not_equal, fill=1.0, base=0,
                                    pattern=[[-1, P]], channel_multiplier=1).then_inc(id_ready, 1)
            for k in range(2):
                pool.dma_start(xin[:, k], t["x"][k]).then_inc(x_in[k], 16)
            pool.wait_ge(gs_in, 16)
            pool.wait_ge(cols_in, 64)
            with pool.Fori(0, NC // 2) as b:
                for k in range(2):
                    c = 2 * b + k
                    for half in range(2):
                        pool.wait_ge(ve_ready, 2 * c + half + 1)
                        nc.gpsimd.tensor_tensor(rs[:], ve[:], mhalf[:], ALU.pow).then_inc(rs_ready, 1)
                        if half == 0:
                            for j in range(TB):
                                pool.wait_ge(n1_ready, TB * c + j + 1)
                                nc.gpsimd.tensor_tensor(xin[:, k, j, :], xin[:, k, j, :], shift[:],
                                                        ALU.add).then_inc(x1_ready, 1)
                    pool.wait_ge(x1_ready, TB * c + TB)
                    pool.wait_ge(xsk_out, 16 * c)
                    for j in range(TB):
                        last = nc.gpsimd.tensor_tensor(xsk[:, j, :], xin[:, k, j, :], bfb[:], ALU.add)
                    last.then_inc(xsk_ready, 1)
                    pool.wait_ge(xsk_ready, c + 1)
                    pool.dma_start(scratch["xs"][c], xsk[:]).then_inc(xsk_out, 16)
                    pool.wait_ge(n2_ready, TB * (c + 1))
                    pool.dma_start(xin[:, k], t["x"][c + 2]).then_inc(x_in[k], 16)
            for k in range(2):
                pool.wait_ge(x_in[k], 16 * (NC // 2 + 1))
            pool.wait_ge(xsk_out, 16 * NC)

        @block.scalar
        def _(act):
            act.dma_start(wada, t["wadaT"]).then_inc(wada_in, 16)
            nc.scalar.preload_act_table_set("natural_log_exp_and_others")
            act.wait_ge(cc_step, 1)
            nc.scalar.activation(cc[:], cc[:], ACT.Exp, scale=-1.0).then_inc(cc_step, 1)
            act.wait_ge(cc_step, 2)
            nc.scalar.activation(cc[:], cc[:], ACT.Ln, bias=1.0).then_inc(cc_step, 1)
            act.wait_ge(cc_step, 3)
            nc.scalar.activation(cc[:], cc[:], ACT.Exp, scale=-1.0).then_inc(cc_step, 1)
            act.wait_ge(fold_in, 64)
            nc.scalar.activation(par[:, :, :, PA:PA + N].rearrange("p a e n -> p (a e) n"),
                                 par[:, :, :, PA:PA + N].rearrange("p a e n -> p (a e) n"),
                                 ACT.Exp).then_inc(par_ready, 1)
            for f in range(NF + 1):
                if f < NF:
                    act.wait_ge(fold_mm, f + 1)
                    if f >= 2:
                        act.wait_ge(wczt_mm, f - 1)
                    nc.scalar.activation(wcz[:, f % 2, :], ps[f % 2][:], ACT.Copy).then_inc(wcz_ready, 1)
                    act.wait_ge(bias_mm, f + 1)
                    bcz = par[:, f // ET, f % ET, PBZ:PBZ + 1]
                    nc.scalar.activation(bcz, ps[4][:, f:f + 1], ACT.Identity, bias=bcz).then_inc(bcz_ready, 1)
                if f >= 1:
                    act.wait_ge(wczt_mm, f)
                    if f >= 3:
                        act.wait_ge(wcz_out[(f - 1) % 2], 16 * ((f - 1) // 2))
                    nc.scalar.activation(wczt[:, (f - 1) % 2, :], ps[2 + (f - 1) % 2][:], ACT.Copy).then_inc(wczt_ready, 1)
            act.wait_ge(cols_in, 64)
            for c in range(NC):
                if c >= 2:
                    act.wait_ge(dbc_mm, 2 * (c - 1))
                    act.wait_ge(xnt_out[c % 2], 16 * (c // 2))
                for d in range(DT):
                    act.wait_ge(xnt_mm, DT * c + d + 1)
                    nc.scalar.activation(xnt[:, c % 2, d, :], ps[d][:], ACT.Identity, scale=cols[:, 0, d:d + 1],
                                         bias=cols[:, 1, d:d + 1]).then_inc(xnt_ready, 1)

        @block.vector
        def _(dve):
            dve.wait_ge(c_in, 16)
            nc.vector.tensor_scalar(cc[:], ct[:], LOW, None, ALU.max).then_inc(cc_step, 1)
            dve.wait_ge(cc_step, 4)
            nc.vector.tensor_tensor(ct[:], ct[:], cc[:], ALU.mult).then_inc(silu_ready, 1)
            dve.wait_ge(par_ready, 1)
            nc.vector.tensor_scalar(par[:, :, :, PA:PA + N].rearrange("p a e n -> p (a e) n"),
                                    par[:, :, :, PA:PA + N].rearrange("p a e n -> p (a e) n"),
                                    -1.0, None, ALU.mult).then_inc(par_ready, 1)
            dve.wait_ge(ada_mm, 3)
            dve.wait_ge(rows_in, 64)
            nc.vector.scalar_tensor_tensor(out=rows[:, 3, :], in0=ps[1][0:B, :], scalar=1.0, in1=rows[:, 3, :],
                                           op0=ALU.add, op1=ALU.add).then_inc(row_step, 1)
            nc.vector.tensor_tensor(rows[:, 2, :], ps[0][0:B, :], rows[:, 2, :], ALU.add).then_inc(row_step, 1)
            dve.wait_ge(row_step, 2)
            nc.vector.tensor_tensor(rows[:, 4, :], rows[:, 0, :], rows[:, 3, :], ALU.mult)
            nc.vector.tensor_tensor(rows[:, 1, :], rows[:, 1, :], rows[:, 3, :], ALU.mult).then_inc(row_step, 1)
            dve.wait_ge(row_step, 3)
            nc.vector.tensor_tensor(rows[:, 5, :], rows[:, 1, :], rows[:, 2, :], ALU.add).then_inc(row_step, 1)
            dve.wait_ge(cols_in, 64)
            for d in range(DT):
                nc.vector.tensor_scalar(gate[:, :, d], ps[7][:, d * B:(d + 1) * B], cols[:, 2, d:d + 1], None,
                                        ALU.add).then_inc(gate_ready, 1)
            dve.wait_ge(gs_in, 16)

            def normalise(c, b, k):
                for half in range(2):
                    for j in range(TB):
                        if half == 0 and j == 0:
                            dve.wait_ge(x_in[k], 16 * (b + 1))
                        if half == 1:
                            dve.wait_ge(x1_ready, TB * c + j + 1)
                        nc.vector.bn_stats(st[:, j, :], xin[:, k, j, :]).then_inc(stats_step, 1)
                    dve.wait_ge(stats_step, 16 * c + 8 * half + TB)
                    nc.vector.memset(pad[:], 0.0)
                    for j in range(TB):
                        nc.vector.bn_aggr(mv[:, j, :], st[:, j, :]).then_inc(stats_step, 1)
                    dve.wait_ge(stats_step, 16 * c + 8 * half + 8)
                    nc.vector.tensor_scalar(ve[:], mv[:, :, 1], EPS, None, ALU.add).then_inc(ve_ready, 1)
                    dve.wait_ge(rs_ready, 2 * c + half + 1)
                    for j in range(TB):
                        if half == 0:
                            nc.vector.tensor_scalar(xin[:, k, j, :], xin[:, k, j, :], mv[:, j, 0:1], rs[:, j:j + 1],
                                                    ALU.subtract, ALU.mult).then_inc(n0_ready, 1)
                        else:
                            nc.vector.tensor_scalar(xn2[:, bass.ds(TB * c + j, 1), :], xin[:, k, j, :], mv[:, j, 0:1],
                                                    rs[:, j:j + 1], ALU.subtract, ALU.mult).then_inc(n2_ready, 1)
                    if half == 0:
                        for j in range(TB):
                            dve.wait_ge(n0_ready, TB * c + j + 1)
                            nc.vector.tensor_tensor(xin[:, k, j, :], xin[:, k, j, :], gs[:, bass.ds(b, 1), 0, :],
                                                    ALU.mult).then_inc(n1_ready, 1)

            with dve.Fori(0, NC // 2) as b:
                nc.vector.tensor_copy(shift[:], gs[:, bass.ds(b, 1), 1, :])
                for k in range(2):
                    normalise(2 * b + k, b, k)
            for d in range(2):
                dve.wait_ge(wczt_mm, ET * (d + 1))
                nc.vector.tensor_copy(wproj[:, d].rearrange("p a r -> p (a r)"), ps[5 + d][:, 0:DT * RD]).then_inc(proj_ready, 1)
            nc.vector.tensor_copy(dbias[:], ps[7][0:RD, 32:34]).then_inc(bias_ready, 1)
            dve.wait_ge(bias_ready, 1)
            for c in range(NC):
                for d in range(2):
                    dve.wait_ge(dbc_mm, 2 * c + d + 1)
                    if c >= 1:
                        dve.wait_ge(dbo_out[d], 32 * (c + (1 if c == NC - 1 else 0)))
                    nc.vector.tensor_scalar(dbo[:, d, :], ps[4 + d][0:RD, :], dbias[:, d:d + 1], None,
                                            ALU.add).then_inc(dbo_ready, 1)

        @block.tensor
        def _(pe):
            pe.wait_ge(silu_ready, 1)
            pe.wait_ge(wada_in, 16)
            for d in range(DT):
                for k in range(KE):
                    last = nc.tensor.matmul(ps[7][:, d * B:(d + 1) * B], wada[:, k, 2 * D + d * P:2 * D + (d + 1) * P],
                                            ct[:, k * B:(k + 1) * B], start=(k == 0), stop=(k == KE - 1))
            last.then_inc(ada_mm, 1)
            for m in range(2):
                for k in range(KE):
                    last = nc.tensor.matmul(ps[m][0:B, :], ct[:, k * B:(k + 1) * B], wada[:, k, m * D:(m + 1) * D],
                                            start=(k == 0), stop=(k == KE - 1))
                last.then_inc(ada_mm, 1)
            pe.wait_ge(fold_in, 64)
            pe.wait_ge(id_ready, 2)
            pe.wait_ge(row_step, 2)

            def transposed(f):
                d, e = f // ET, f % ET
                pe.wait_ge(wcz_ready, f + 1)
                if f >= 2:
                    pe.wait_ge(wczt_ready, f - 1)
                for k in range(DT):
                    last = nc.tensor.matmul(ps[2 + f % 2][:, k * P:(k + 1) * P], wcz[:, f % 2, k * P:(k + 1) * P],
                                            ident[:], start=True, stop=True, is_transpose=True)
                for k in range(DT):
                    nc.tensor.matmul(ps[5 + d][:, k * RD:(k + 1) * RD], wcz[:, f % 2, k * P:(k + 1) * P],
                                     wdbc[:, d, e, :], start=(e == 0 and k == 0), stop=(e == ET - 1),
                                     skip_group_check=True)
                pe.wait_ge(bcz_ready, f + 1)
                last = nc.tensor.matmul(ps[7][0:RD, 32 + d:33 + d], wdbc[:, d, e, :], par[:, d, e, PBZ:PBZ + 1],
                                        start=(e == 0), stop=(e == ET - 1), skip_group_check=True)
                last.then_inc(wczt_mm, 1)

            pe.wait_ge(gate_ready, DT)
            for f in range(NF + 1):
                if f < NF:
                    pe.wait_ge(wct_in[f % 2], 16 * (f // 2 + 1))
                    if f >= 2:
                        pe.wait_ge(wcz_ready, f - 1)
                    for k in range(KE):
                        last = nc.tensor.matmul(ps[f % 2][:], wct[:, f % 2, k, :], wz[:, k, :],
                                                start=(k == 0), stop=(k == KE - 1))
                    last.then_inc(fold_mm, 1)
                if f >= 1:
                    transposed(f - 1)
                if f < NF:
                    for k in range(KE):
                        last = nc.tensor.matmul(ps[4][:, f:f + 1], wct[:, f % 2, k, :], bz[:, k:k + 1],
                                                start=(k == 0), stop=(k == KE - 1), skip_group_check=True)
                    last.then_inc(bias_mm, 1)
            pe.wait_ge(wczt_ready, NF)
            for c in range(NC):
                pe.wait_ge(n2_ready, TB * (c + 1))
                for d in range(DT):
                    if c >= 1:
                        pe.wait_ge(xnt_ready, DT * (c - 1) + d + 1)
                    for j in range(TB):
                        last = nc.tensor.matmul(ps[d][:, j * P:(j + 1) * P], xn2[:, TB * c + j, d * P:(d + 1) * P],
                                                ident[:], start=True, stop=True, is_transpose=True)
                    last.then_inc(xnt_mm, 1)
                pe.wait_ge(xnt_ready, DT * (c + 1))
                pe.wait_ge(proj_ready, 2)
                for d in range(2):
                    if c >= 1:
                        pe.wait_ge(dbo_ready, 2 * (c - 1) + d + 1)
                    for k in range(DT):
                        last = nc.tensor.matmul(ps[4 + d][0:RD, :], wproj[:, d, k, :], xnt[:, c % 2, k, :],
                                                start=(k == 0), stop=(k == DT - 1))
                    last.then_inc(dbc_mm, 1)


def ssm_kernel(nc, t, scratch):
    with ExitStack() as ctx:
        def sb(name, shape):
            return ctx.enter_context(nc.sbuf_tensor(name, shape, fp32))

        def sem(name):
            return ctx.enter_context(nc.semaphore(name))

        gate, ident = t["gate"], t["ident"]
        bcb = sb("bcb", [P, 2, GR, NG, TC])
        decay = sb("decay", [P, 2, NG, TC])
        state = sb("state", [P, GR, NG, TC])
        xn = sb("xn", [P, 2, DT, TC])
        dl = sb("dl", [R, 2, TC])
        wzs = sb("wzs", [P, 2, D])
        wdt = sb("wdt", [R, 2, P])
        wtail = sb("wtail", [P, 2, D])
        par = sb("upar", [P, 2, NP_])
        u, delta, du, ud = (sb(n, [P, 2, TC]) for n in ("u", "delta", "du", "ud"))
        soft = sb("soft", [P, TC])
        mx, sig = (sb(n, [P, TC]) for n in ("mx", "sig"))
        ym = sb("ym", [P, 2, 2, TC])
        ygate = sb("ygate", [P, 2, TC])
        xskip = sb("xskip", [P, TB, D])
        res = sb("res", [P, DT, TC])
        carry = sb("carry", [P, ET * N])
        first_state = sb("first_state", [P, 2, N])
        yps = [ctx.enter_context(nc.psum_tensor(f"yps{j}", [P, TC], fp32)) for j in range(2)]
        zps = ctx.enter_context(nc.psum_tensor("zps", [P, TC], fp32))
        dps = ctx.enter_context(nc.psum_tensor("dps", [P, TC], fp32))
        ops = [ctx.enter_context(nc.psum_tensor(f"ops{d}", [P, TC], fp32)) for d in range(DT)]

        unit_in, tail_in, xn_in, ym_in, ym_out = ([sem(f"{n}{j}") for j in range(2)] for n in (
            "unit_in", "tail_in", "xn_in", "ym_in", "ym_out"))
        b_in = [sem(f"b_in{g}") for g in range(GR)]
        c_in = [sem(f"c_in{g}") for g in range(GR)]
        xskip_in, res_in, res_out = sem("xskip_in"), sem("res_in"), sem("res_out")
        z_mm, d_mm, group_done, tr_mm, tail_mm, init_mm = (sem(n) for n in (
            "z_mm", "d_mm", "group_done", "tr_mm", "tail_mm", "init_mm"))
        u_ready, d_read, soft_step, soft_ready, ud_ready, decay_ready, mx_ready, sig_step, sig_ready = (
            sem(n) for n in ("u_ready", "d_read", "soft_step", "soft_ready", "ud_ready", "decay_ready",
                             "mx_ready", "sig_step", "sig_ready"))
        delta_ready, du_ready, scanned, prod_ready, y_read, clamp_ready, act_ready, y_ready, res_ready = (
            sem(n) for n in ("delta_ready", "du_ready", "scanned", "prod_ready", "y_read",
                             "clamp_ready", "act_ready", "y_ready", "res_ready"))
        carried, saved, dbu_ready = sem("carried"), sem("saved"), sem("dbu_ready")
        block = ctx.enter_context(nc.Block())

        def done(count):
            return value(count + 1)

        class Unit:
            def __init__(self, b, s, i, n):
                def count(per_b, per_i, c):
                    return Count(b, i, per_b, per_i if n in (1, 2) else 0, c)

                self.b, self.s = count(1, 0, 0), s
                self.first, self.last = n == 0, n == ET - 1
                self.j = n % 2
                self.backward = s >= 2
                tile = count(0, 2, n)
                pair = count(0, 1, n // 2)
                self.tile = tile
                self.q = tile + count(UPB, 0, s * ET)
                self.qs = pair + count(UPB // 2, 0, s * (ET // 2))
                self.f = tile + count(2 * ET, 0, s * ET)
                self.v = tile + count(2 * ET, 0, (s - 2) * ET)
                self.w = count(2, 0, s - 2)
                self.direction = count(2, 0, s // 2)
                self.next_tile = count(0, 0, 0) if self.last else tile + 1
                self.next_s = (s + 1) % SEGS if self.last else s
                self.next_qs = self.qs + self.j
                self.prev_s = s - 1 if self.first else s
                self.has_prev = not (self.first and s == 0)
                self.prev_forward = self.has_prev and self.prev_s < 2
                self.prev_backward = self.has_prev and self.prev_s >= 2
                self.prev_tile = count(0, 0, ET - 1) if self.first else tile - 1
                self.prev_qs = self.qs - (1 - self.j)

        def units(eng, unit):
            with eng.Fori(0, B) as b:
                for s in range(SEGS):
                    unit(Unit(b, s, None, 0))
                    with eng.Fori(0, (ET - 2) // 2) as i:
                        unit(Unit(b, s, i, 1))
                        unit(Unit(b, s, i, 2))
                    unit(Unit(b, s, None, ET - 1))

        @block.sync
        def _(sp):
            for s in (res_out, *ym_out):
                sp.sem_inc(s, 16)

            def row(count):
                v = value(count)
                return v if isinstance(v, int) else sp.snap(v)

            def load_weights(j, tile):
                sp.dma_start(wzs[:, j, :], scratch["wz"][tile]).then_inc(unit_in[j], 16)
                sp.dma_start(wdt[:, j, :], t["wdtT"][tile]).then_inc(unit_in[j], 16)

            def load_parameters(j, tile):
                sp.dma_start(par[:, j, :], scratch["par"][tile]).then_inc(unit_in[j], 16)

            def load_tokens(chunk, s):
                sp.dma_start(xn[:, s % 2], scratch["xn"][chunk]).then_inc(xn_in[s % 2], 16)
                sp.dma_start(dl[:, s % 2, :], scratch["dl"][s // 2, chunk]).then_inc(xn_in[s % 2], 16)

            def load_row_group(which, chunk, s, g):
                rows = scratch["bc"][s // 2, chunk, N * which + NG * g:N * which + NG * (g + 1), :]
                sp.dma_start(bcb[:, which, g].rearrange("p n t -> p (n t)"),
                             rows.rearrange("n t -> (n t)").partition_broadcast(P)
                             ).then_inc((b_in, c_in)[which][g], 16)

            load_weights(0, 0)
            load_parameters(0, 0)
            load_tokens(0, 0)
            for g in range(GR):
                for which in range(2):
                    load_row_group(which, 0, 0, g)

            def reload_rows(which, g, q, chunk, s):
                sp.wait_ge((dbu_ready, prod_ready)[which], value(GR * q + g + 1))
                load_row_group(which, chunk, s, g)

            def unit(x):
                next_row, tile, prev_tile = row(x.next_tile + (x.next_s // 2) * ET), row(x.tile), row(x.prev_tile)
                chunk, before = row(x.b * 2 + HALF[x.s]), row(x.b * 2 + HALF[x.s - 1])
                nxt = row(x.b * 2 + (HALF[x.s + 1] if x.s < SEGS - 1 else 2))
                mx_done, tails = row(x.f + 1), row(x.q + 1 if x.first and x.s == 0 else x.q)
                stored = row(x.f + 1)
                sp.wait_ge(decay_ready, done(GR * x.q))
                load_weights(1 - x.j, next_row)
                if x.prev_forward:
                    sp.wait_ge(mx_ready, mx_done)
                load_parameters(1 - x.j, next_row)
                sp.wait_ge(tail_mm, tails)
                sp.dma_start(wtail[:, x.j, :], t["wfT" if x.backward else "wxT"][tile]).then_inc(tail_in[x.j], 16)
                if x.first:
                    if x.has_prev:
                        for g in (2, 3):
                            reload_rows(1, g, x.q - 1, chunk, x.s)
                    sp.wait_ge(z_mm, value(x.q + 2))
                    load_tokens(nxt, (x.s + 1) % SEGS)
                    if x.backward:
                        sp.wait_ge(init_mm, done(x.w))
                        sp.dma_start(xskip[:], scratch["xs"][chunk]).then_inc(xskip_in, 16)
                if x.last:
                    for which, g in ((0, 0), (0, 1), (0, 2), (0, 3), (1, 0), (1, 1)):
                        reload_rows(which, g, x.q, nxt, (x.s + 1) % SEGS)
                if x.prev_forward:
                    sp.wait_ge(act_ready, stored)
                    sp.dma_start(scratch["ym"][HALF[x.prev_s], prev_tile],
                                 ym[:, 1 - x.j]).then_inc(ym_out[1 - x.j], 16)
                if x.backward:
                    if x.first and x.s == 2:
                        sp.wait_ge(ym_out[x.j], value(16 * (x.b * ET + ET + 1)))
                    elif x.s == 2 and x.tile.c == 1:
                        sp.wait_ge(ym_out[x.j], value(16 * (x.b * ET + ET + 1)))
                    else:
                        sp.wait_ge(y_ready, done(x.v - 1))
                    sp.dma_start(ym[:, x.j], scratch["ym"][HALF[x.s], tile]).then_inc(ym_in[x.j], 16)
                if x.first and x.s == 3:
                    store_result(before, x.w)
                if x.last:
                    if x.backward:
                        sp.wait_ge(res_out, value(16 * (x.w + 1)))
                        sp.dma_start(res[:], t["xT"][chunk]).then_inc(res_in, 16)
                    if x.s == 3:
                        for g in (2, 3):
                            reload_rows(1, g, x.q, nxt, 0)
                        store_result(chunk, x.w + 1)

            def store_result(chunk, segments):
                sp.wait_ge(res_ready, done(DT * segments))
                sp.dma_start(t["out"][chunk], res[:]).then_inc(res_out, 16)

            units(sp, unit)
            sp.wait_ge(res_out, 16 * (2 * B + 1))
            sp.wait_ge(unit_in[0], 48 * (UPB * B // 2 + 1))
            sp.wait_ge(xn_in[0], 32 * (2 * B + 1))
            for g in range(GR):
                sp.wait_ge(b_in[g], 16 * (SEGS * B + 1))
                sp.wait_ge(c_in[g], 16 * (SEGS * B + 1))

        @block.tensor
        def _(pe):
            pe.sem_inc(group_done, GR)
            for s in (tail_mm, init_mm, tr_mm):
                pe.sem_inc(s, 1)

            def delta_product(j, s, q, qs, b_seg):
                pe.wait_ge(unit_in[j], value(48 * (qs + 1)))
                pe.wait_ge(xn_in[s % 2], value(32 * (b_seg + 1)))
                pe.wait_ge(d_read, done(q))
                nc.tensor.matmul(dps[:], wdt[:, j, :], dl[:, s % 2, :], start=True, stop=True).then_inc(d_mm, 1)

            def z_product(j, s):
                for k in range(DT):
                    last = nc.tensor.matmul(zps[:], wzs[:, j, k * P:(k + 1) * P], xn[:, s % 2, k, :],
                                            start=(k == 0), stop=(k == DT - 1))
                last.then_inc(z_mm, 1)

            def transpose_y(j, q):
                pe.wait_ge(y_read, value(q + 3))
                for k in range(TB):
                    last = nc.tensor.matmul(zps[:, k * P:(k + 1) * P], ym[:, j, 0, k * P:(k + 1) * P], ident[:],
                                            start=True, stop=True, is_transpose=True)
                last.then_inc(tr_mm, 1)

            def project(j, v, qs, stop):
                pe.wait_ge(tail_in[j], value(16 * (qs + 1)))
                pe.wait_ge(y_ready, done(v + 1))
                for d in range(DT):
                    last = nc.tensor.matmul(ops[d][:], wtail[:, j, d * P:(d + 1) * P], ygate[:, j, :],
                                            start=False, stop=stop, skip_group_check=True)
                last.then_inc(tail_mm, 1)

            def transpose_group(j, q, g):
                pe.wait_ge(prod_ready, value(GR * q + g + 1))
                for n in range(NG):
                    for k in range(TB):
                        last = nc.tensor.matmul(yps[j][:, k * P:(k + 1) * P], state[:, g, n, k * P:(k + 1) * P],
                                                ident[:], start=False, stop=(g == GR - 1 and n == NG - 1),
                                                is_transpose=True, skip_group_check=True)
                last.then_inc(group_done, 1)

            def unit(x):
                pairs = x.b * 2 + (x.s // 2) if not x.last else x.b * 2 + ((x.s + 1) // 2)
                delta_product(1 - x.j, x.next_s, x.q + 1, x.next_qs, pairs)
                if x.has_prev:
                    transpose_group(1 - x.j, x.q - 1, GR - 1)
                pe.wait_ge(u_ready, done(x.q + 1))
                if x.first and x.s == 0:
                    pe.wait_ge(y_ready, done(2 * ET * x.b))
                elif x.prev_forward:
                    pe.wait_ge(mx_ready, done(x.f))
                else:
                    pe.wait_ge(y_ready, done(x.v - 1))
                z_product(1 - x.j, x.next_s)
                for g in range(GR):
                    if g == 0:
                        pe.wait_ge(ud_ready, value(x.q + 1))
                        pe.wait_ge(y_read, value(x.q + 1))
                        for k in range(TB):
                            nc.tensor.matmul(yps[x.j][:, k * P:(k + 1) * P], ud[:, x.j, k * P:(k + 1) * P], ident[:],
                                             start=(k == 0), stop=False, is_transpose=True, skip_group_check=True)
                    if g < GR - 1 or x.last and x.s == 3:
                        transpose_group(x.j, x.q, g)
                    if g == 0 and (x.prev_backward or not x.backward):
                        pe.wait_ge(u_ready, done(x.q + 2))
                    if g == 0 and x.prev_backward:
                        transpose_y(1 - x.j, x.q - 1)
                    if g == 0 and not x.backward:
                        pe.wait_ge(tail_in[x.j], value(16 * (x.qs + 1)))
                        for k in range(DT):
                            last = nc.tensor.matmul(zps[:], wtail[:, x.j, k * P:(k + 1) * P], xn[:, x.s % 2, k, :],
                                                    start=(k == 0), stop=(k == DT - 1))
                        last.then_inc(tail_mm, 1)
                    if g == 1 and x.prev_backward:
                        project(1 - x.j, x.v - 1, x.prev_qs, x.first)
                if x.first and x.backward:
                    pe.wait_ge(res_ready, done(DT * x.w))
                    pe.wait_ge(xskip_in, value(16 * (x.w + 1)))
                    for d in range(DT):
                        for k in range(TB):
                            last = nc.tensor.matmul(ops[d][:, k * P:(k + 1) * P], xskip[:, k, d * P:(d + 1) * P],
                                                    ident[:], start=(k == 0), stop=False, is_transpose=True,
                                                    skip_group_check=True)
                    last.then_inc(init_mm, 1)
                if x.last and x.s == 3:
                    transpose_y(x.j, x.q)
                    project(x.j, x.v, x.qs, True)

            delta_product(0, 0, 0, 0, 0)
            z_product(0, 0)
            units(pe, unit)

        @block.scalar
        def _(act):
            nc.scalar.preload_act_table_set("natural_log_exp_and_others")
            for s in (d_read, u_ready, decay_ready, mx_ready):
                act.sem_inc(s, 1)

            def start_delta(j, q, qs):
                act.wait_ge(unit_in[j], value(48 * (qs + 1)))
                act.wait_ge(d_mm, value(q + 1))
                nc.scalar.activation(soft[:], dps[:], ACT.Abs, bias=par[:, j, PBD:PBD + 1]).then_inc(soft_step, 1)
                nc.scalar.activation(delta[:, j, :], dps[:], ACT.Relu, bias=par[:, j, PBD:PBD + 1]).then_inc(d_read, 1)

            def finish_soft(j, q):
                act.wait_ge(soft_step, value(2 * q + 1))
                nc.scalar.activation(soft[:], soft[:], ACT.Exp, scale=-1.0).then_inc(soft_step, 1)
                act.wait_ge(z_mm, value(q + 1))
                nc.scalar.activation(u[:, j, :], zps[:], ACT.Identity, bias=par[:, j, PBZ:PBZ + 1]).then_inc(u_ready, 1)
                act.wait_ge(soft_step, value(2 * q + 2))
                nc.scalar.activation(soft[:], soft[:], ACT.Ln, bias=1.0).then_inc(soft_ready, 1)
                act.wait_ge(u_ready, done(q + 1))
                if q != 0:
                    act.wait_ge(group_done, value(GR * q))
                nc.scalar.activation(ud[:, j, :], u[:, j, :], ACT.Copy, scale=par[:, j, PDP:PDP + 1]).then_inc(ud_ready, 1)

            def unit(x):
                for g in range(GR):
                    if g == 0:
                        act.wait_ge(delta_ready, value(x.q + 1))
                    act.wait_ge(scanned, value(GR * x.q + g + 1))
                    for n in range(NG):
                        m = NG * g + n
                        last = nc.scalar.activation(decay[:, g % 2, n, :], delta[:, x.j, :], ACT.Exp,
                                                    scale=par[:, x.j, PA + m:PA + m + 1])
                    last.then_inc(decay_ready, 1)
                    if g == 1:
                        act.wait_ge(decay_ready, done(GR * x.q))
                        start_delta(1 - x.j, x.q + 1, x.next_qs)
                    if g == 2:
                        finish_soft(1 - x.j, x.q + 1)
                    if g == 2 and x.prev_forward:
                        if x.prev_s == 0:
                            act.wait_ge(y_ready, done(2 * ET * x.b))
                        act.wait_ge(ym_out[1 - x.j], value(16 * (x.prev_qs - x.b * ET + 1)))
                        act.wait_ge(group_done, value(GR * (x.q + 1)))
                        act.wait_ge(y_read, value(x.q + 1))
                        nc.scalar.activation(ym[:, 1 - x.j, 0, :], yps[1 - x.j][:], ACT.Copy).then_inc(y_read, 1)
                        act.wait_ge(clamp_ready, value(x.f))
                        nc.scalar.activation(sig[:], sig[:], ACT.Exp, scale=-1.0).then_inc(sig_step, 1)
                        act.wait_ge(sig_step, value(2 * x.f - 1))
                        nc.scalar.activation(sig[:], sig[:], ACT.Ln, bias=1.0).then_inc(sig_step, 1)
                        act.wait_ge(sig_step, value(2 * x.f))
                        nc.scalar.activation(sig[:], sig[:], ACT.Exp, scale=-1.0).then_inc(sig_ready, 1)
                if not x.backward:
                    act.wait_ge(tail_mm, done(x.q + 1))
                    act.wait_ge(act_ready, done(x.f))
                    nc.scalar.activation(mx[:], zps[:], ACT.Identity, bias=par[:, x.j, PBX:PBX + 1]).then_inc(mx_ready, 1)

            start_delta(0, 0, 0)
            finish_soft(0, 0)
            units(act, unit)

        @block.gpsimd
        def _(pool):
            def unit(x):
                for g in range(GR):
                    if g == 0:
                        pool.wait_ge(du_ready, done(x.q + 1))
                    pool.wait_ge(b_in[g], value(16 * (x.b * SEGS + x.s + 1)))
                    pool.wait_ge(group_done, value(GR * x.q + g + 1))
                    nc.gpsimd.tensor_tensor(state[:, g], bcb[:, 0, g],
                                            du[:, x.j:x.j + 1, :].broadcast_to([P, NG, TC]),
                                            ALU.mult).then_inc(dbu_ready, 1)

            units(pool, unit)

        @block.vector
        def _(dve):
            dve.sem_inc(scanned, 2)
            dve.sem_inc(y_read, 2)
            for s in (du_ready, act_ready, y_ready, res_ready, carried):
                dve.sem_inc(s, 1)

            def finish_delta(j, q):
                dve.wait_ge(soft_ready, value(q + 1))
                nc.vector.tensor_tensor(delta[:, j, :], delta[:, j, :], soft[:], ALU.add).then_inc(delta_ready, 1)

            def finish_du(j, q):
                dve.wait_ge(delta_ready, value(q + 1))
                dve.wait_ge(u_ready, done(q + 1))
                nc.vector.tensor_tensor(du[:, j, :], delta[:, j, :], u[:, j, :], ALU.mult).then_inc(du_ready, 1)

            def sum_y(j, q, qs, b):
                dve.wait_ge(group_done, value(GR * (q + 2)))
                dve.wait_ge(ym_in[j], value(16 * (qs - b * ET - ET + 1)))
                dve.wait_ge(y_read, value(q + 2))
                nc.vector.tensor_tensor(ym[:, j, 0, :], yps[j][:], ym[:, j, 0, :], ALU.add).then_inc(y_read, 1)

            def gate_y(j, v, tails):
                dve.wait_ge(tr_mm, done(v + 1))
                dve.wait_ge(tail_mm, done(tails))
                nc.vector.tensor_tensor(ygate[:, j, :], zps[:], ym[:, j, 1, :], ALU.mult).then_inc(y_ready, 1)

            def results(b, w, tails):
                dve.wait_ge(tail_mm, done(tails))
                dve.wait_ge(res_in, value(16 * (w + 1)))
                for d in range(DT):
                    nc.vector.scalar_tensor_tensor(out=res[:, d, :], in0=ops[d][:], scalar=gate[:, bass.ds(value(b), 1), d],
                                                   in1=res[:, d, :], op0=ALU.mult, op1=ALU.add).then_inc(res_ready, 1)

            def unit(x):
                step = -1 if x.backward else 1
                second = x.s % 2 == 1
                firsts = x.direction * ET + x.tile

                def scan(g, n):
                    m = NG * g + n
                    h = state[:, g, n, ::step]
                    return nc.vector.tensor_tensor_scan(h, decay[:, g % 2, n, ::step], h,
                                                        first_state[:, x.j, m:m + 1] if second else 0.0,
                                                        ALU.mult, ALU.add)

                def save_carry(g):
                    edge = 0 if x.backward else TC - 1
                    dve.wait_ge(scanned, value(GR * x.q + g + 3))
                    if x.first and g == 0:
                        dve.wait_ge(carried, done(ET * x.direction))
                    nc.vector.tensor_copy(carry[:, bass.ds(value(x.tile * N + NG * g), NG)],
                                          state[:, g, :, edge]).then_inc(saved, 1)

                def product(g):
                    dve.wait_ge(c_in[g], value(16 * (x.b * SEGS + x.s + 1)))
                    dve.wait_ge(scanned, value(GR * x.q + g + 3))
                    if not second:
                        dve.wait_ge(saved, value(firsts * GR + g + 1))
                    nc.vector.tensor_tensor(state[:, g], state[:, g], bcb[:, 1, g], ALU.mult).then_inc(prod_ready, 1)

                if second:
                    dve.wait_ge(carried, done(firsts + 1))
                for g in range(GR):
                    dve.wait_ge(decay_ready, done(GR * x.q + g + 1))
                    dve.wait_ge(dbu_ready, value(GR * x.q + g + 1))
                    scan(g, 0)
                    if g > 0 and not second:
                        save_carry(g - 1)
                    for n in range(1, NG):
                        last = scan(g, n)
                    last.then_inc(scanned, 1)
                    if g == 0 and x.prev_forward:
                        dve.wait_ge(mx_ready, done(x.f))
                        dve.wait_ge(act_ready, done(x.f - 1))
                        nc.vector.tensor_scalar(sig[:], mx[:], LOW, None, ALU.max).then_inc(clamp_ready, 1)
                    if g == 1 and x.prev_backward:
                        sum_y(1 - x.j, x.q - 1, x.prev_qs, x.b)
                    if g == 2:
                        finish_delta(1 - x.j, x.q + 1)
                        if x.prev_backward:
                            gate_y(1 - x.j, x.v - 1, x.q - 2)
                        finish_du(1 - x.j, x.q + 1)
                    if g == 3 and x.prev_forward:
                        if x.prev_s == 0:
                            dve.wait_ge(y_ready, done(2 * ET * x.b))
                        dve.wait_ge(ym_out[1 - x.j], value(16 * (x.prev_qs - x.b * ET + 1)))
                        dve.wait_ge(sig_ready, value(x.f))
                        nc.vector.tensor_tensor(ym[:, 1 - x.j, 1, :], mx[:], sig[:], ALU.mult).then_inc(act_ready, 1)
                    if g > 0:
                        product(g - 1)
                if x.next_s % 2 == 1:
                    later = x.b * 2 + x.next_s // 2
                    dve.wait_ge(saved, value((later * ET + x.next_tile + 1) * GR))
                    dve.wait_ge(scanned, value(GR * x.q + 2))
                    nc.vector.tensor_copy(first_state[:, 1 - x.j, :],
                                          carry[:, bass.ds(value(x.next_tile * N), N)]).then_inc(carried, 1)
                if not second:
                    save_carry(GR - 1)
                product(GR - 1)
                if x.first and x.s == 3:
                    results(x.b, x.w - 1, x.q)
                if x.last and x.s == 3:
                    sum_y(x.j, x.q, x.qs, x.b)
                    gate_y(x.j, x.v, x.q - 1)
                    results(x.b, x.w, x.q + 1)

            finish_delta(0, 0)
            finish_du(0, 0)
            units(dve, unit)


def build(nc, t):
    with ExitStack() as ctx:
        scratch = {
            "gs": nc.dram_tensor("gs_s", (B, 2, D), fp32).ap(),
            "wz": nc.dram_tensor("wz_s", (2 * ET, P, D), fp32).ap(),
            "par": nc.dram_tensor("par_s", (2 * ET, P, NP_), fp32).ap(),
            "xn": nc.dram_tensor("xn_s", (NC + 1, P, DT, TC), fp32).ap(),
            "dl": nc.dram_tensor("dl_s", (2, NC + 1, R, TC), fp32).ap(),
            "bc": nc.dram_tensor("bc_s", (2, NC + 1, 2 * N, TC), fp32).ap(),
            "xs": nc.dram_tensor("xs_s", (NC, P, TB, D), fp32).ap(),
            "ym": nc.dram_tensor("ym_s", (2, ET, P, 2, TC), fp32).ap(),
        }
        t["gate"] = ctx.enter_context(nc.sbuf_tensor("gate", [P, B, DT], fp32))
        t["ident"] = ctx.enter_context(nc.sbuf_tensor("ident", [P, P], fp32))
        setup_kernel(nc, t, scratch)
        ssm_kernel(nc, t, scratch)


def kernel(**inputs):
    import numpy as np
    import concourse.bacc as bacc
    from concourse.bass_utils import run_bass_kernel_spmd

    a = {k.replace("L0_cond_", ""): np.asarray(v) for k, v in inputs.items()}

    def tiles(m):
        return m.reshape(m.shape[0] // P, P, *m.shape[1:]).swapaxes(0, 1)

    x = a["x"]
    xc = x.reshape(NC, TB, P, D).transpose(0, 2, 1, 3)
    par = np.concatenate([np.concatenate([
        tiles(a[f"Alog{d}"]),
        *(tiles(a[n].reshape(E, 1)) for n in (f"bc{d}", f"bdt{d}", f"Dp{d}", "bx"))], axis=2)[:, None]
        for d in (1, 2)], axis=1)
    arrays = {
        "x": np.concatenate([xc, xc[:2]]),
        "xT": x.reshape(B, 2, TC, DT, P).transpose(0, 1, 4, 3, 2).reshape(NC, P, DT, TC),
        "cT": tiles(a["cond_2048"].T).reshape(P, KE * B),
        "wadaT": tiles(a["Wada"].T),
        "g1": a["norm1_g"], "b1": a["norm1_b"], "bada": a["bada"], "bf": a["bf"],
        "g2": a["norm2_g"].reshape(DT, P).T, "b2": a["norm2_b"].reshape(DT, P).T,
        "bgate": a["bada"][2 * D:].reshape(DT, P).T,
        "Wz": tiles(a["Wz"]), "bz": a["bz"].reshape(KE, P).T,
        "wcT": np.concatenate([a[f"Wc{d}"].reshape(ET, P, KE, P).transpose(0, 3, 2, 1) for d in (1, 2)]),
        "wdbcT": np.stack([tiles(a[f"Wdbc{d}"].T) for d in (1, 2)], axis=1),
        "wdtT": np.concatenate([a[f"Wdt{d}"].reshape(ET, P, R).transpose(0, 2, 1) for d in (1, 2)]),
        "wxT": a["Wx"].reshape(ET, P, DT, P).transpose(0, 3, 2, 1).reshape(ET, P, D),
        "wfT": a["Wf"].T.reshape(ET, P, D),
        "par": par,
    }
    nc = bacc.Bacc("TRN2", target_bir_lowering=False, num_devices=1)
    feed, t = {}, {}
    for name, v in arrays.items():
        v = np.ascontiguousarray(v)
        feed[f"in_{name}"] = v
        t[name] = nc.dram_tensor(f"in_{name}", v.shape, mybir.dt.from_np(v.dtype), kind="ExternalInput").ap()
    t["out"] = nc.dram_tensor("out_t", (NC, P, DT, TC), fp32, kind="ExternalOutput").ap()
    build(nc, t)
    got = run_bass_kernel_spmd(nc, [feed], core_ids=[0])
    return np.ascontiguousarray(got.results[0]["out_t"].transpose(0, 3, 2, 1).reshape(B, S, D))
```

```python
import concourse.bass as bass
from concourse import mybir
from contextlib import ExitStack

fp32 = mybir.dt.float32
ALU = mybir.AluOpType
ACT = mybir.ActivationFunctionType

B, S, D, E, N, R = 4, 1024, 512, 1024, 16, 64
P = 128
TC = 512
NC = B * S // TC
DT = D // P
ET = E // P
KE = E // P
TB = TC // P
NG = 4
GR = N // NG
RD = R + 2 * N
SEGS = 4
HALF = [0, 1, 1, 0]
UPB = SEGS * ET
LOW = -40.0
EPS = 1e-5
PA, PBZ, PBD, PDP, PBX, NP_ = 0, N, N + 1, N + 2, N + 3, N + 4


class Count:

    def __init__(self, b, i, per_b, per_i, c):
        self.b, self.i, self.per_b, self.per_i, self.c = b, i, per_b, per_i, c

    def __add__(self, o):
        if isinstance(o, int):
            return Count(self.b, self.i, self.per_b, self.per_i, self.c + o)
        return Count(self.b, self.i, self.per_b + o.per_b, self.per_i + o.per_i, self.c + o.c)

    def __sub__(self, o):
        return self + o * -1

    def __mul__(self, k):
        return Count(self.b, self.i, self.per_b * k, self.per_i * k, self.c * k)

    __rmul__ = __mul__

    def value(self):
        assert self.c >= 0 and self.per_b >= 0 and self.per_i >= 0
        v = self.c
        if self.per_i:
            v = self.i * self.per_i + v
        if self.per_b:
            v = self.b * self.per_b + v
        return v


def value(x):
    return x if isinstance(x, int) else x.value()


def setup_kernel(nc, t, scratch):
    with ExitStack() as ctx:
        def sb(name, shape):
            return ctx.enter_context(nc.sbuf_tensor(name, shape, fp32))

        def sem(name):
            return ctx.enter_context(nc.semaphore(name))

        gate = t["gate"]
        ident = t["ident"]
        xn2 = sb("xn2", [P, NC * TB, D])
        wada = xn2[:, 0:24, :].rearrange("p a d -> p (a d)").rearrange("p (k m) -> p k m", k=KE)
        wz = sb("wz", [P, KE, D])
        gs = sb("gs", [P, B, 2, D])
        wct = sb("wct", [P, 2, KE, P])
        wcz = sb("wcz", [P, 2, D])
        wczt = sb("wczt", [P, 2, D])
        xin = sb("xin", [P, 2, TB, D])
        xsk = sb("xsk", [P, TB, D])
        wdbc = sb("wdbc", [P, 2, KE, RD])
        wproj = sb("wproj", [P, 2, DT, RD])
        dbo = sb("dbo", [RD, 2, TC])
        bfb = sb("bfb", [P, D])
        par = sb("par", [P, 2, ET, NP_])
        rows = sb("rows", [B, 6, D])
        ct = sb("ct", [P, KE * B])
        cc = sb("cc", [P, KE * B])
        cols = sb("cols", [P, 3, DT])
        bz = sb("bz", [P, KE])
        dbias = sb("dbias", [RD, 2])
        st = sb("st", [P, TB, 6])
        mv = sb("mv", [P, TB, 2])
        ve = sb("ve", [P, TB])
        rs = sb("rs", [P, TB])
        mhalf = sb("mhalf", [P, TB])
        pad = sb("pad", [P, 1])
        gain = sb("gain", [P, D])
        shift = sb("shift", [P, D])
        ps = [ctx.enter_context(nc.psum_tensor(f"ps{i}", [P, TC], fp32)) for i in range(8)]

        c_in, wada_in, rows_in, fold_in, cols_in = (sem(n) for n in
                                                    ("c_in", "wada_in", "rows_in", "fold_in", "cols_in"))
        wz_in = sem("wz_in")
        wct_in = [sem(f"wct_in{j}") for j in range(2)]
        id_ready, gs_out, gs_in, par_out = (sem(n) for n in ("id_ready", "gs_out", "gs_in", "par_out"))
        cc_step, silu_ready, ada_mm, row_step, par_ready = (sem(n) for n in (
            "cc_step", "silu_ready", "ada_mm", "row_step", "par_ready"))
        gate_ready, fold_mm, wcz_ready, bcz_ready, wczt_mm, wczt_ready = (sem(n) for n in (
            "gate_ready", "fold_mm", "wcz_ready", "bcz_ready", "wczt_mm", "wczt_ready"))
        bias_mm = sem("bias_mm")
        wcz_out = [sem(f"wcz_out{j}") for j in range(2)]
        x_in = [sem(f"x_in{j}") for j in range(2)]
        stats_step, ve_ready, rs_ready, gain_ready, n1_ready, x1_ready, xsk_ready, n2_ready, xsk_out = (
            sem(n) for n in ("stats_step", "ve_ready", "rs_ready", "gain_ready", "n1_ready", "x1_ready",
                             "xsk_ready", "n2_ready", "xsk_out"))
        xnt_mm, xnt_ready = sem("xnt_mm"), sem("xnt_ready")
        dbc_mm, dbo_ready, proj_ready = ([sem(f"{n}{d}") for d in range(2)] for n in (
            "dbc_mm", "dbo_ready", "proj_ready"))
        xnt_out = sem("xnt_out")
        dbo_out = [sem(f"dbo_out{j}") for j in range(2)]
        block = ctx.enter_context(nc.Block())

        def xn_tile(c, d):
            return xn2[:, TB * c:TB * (c + 1), d * P:(d + 1) * P]

        NF = 2 * ET
        FA = 3
        FX = NF + 1 - NC

        @block.sync
        def _(sp):
            sp.dma_start(ct[:], t["cT"]).then_inc(c_in, 16)
            def load_small():
                for n, (src, m) in enumerate((("g1", 0), ("b1", 0), ("bada", 0), ("bada", 1))):
                    sp.dma_start(rows[:, n, :], t[src][m * D:(m + 1) * D].partition_broadcast(B)).then_inc(rows_in, 16)
                sp.dma_start(bz[:], t["bz"]).then_inc(fold_in, 16)
                sp.dma_start(wdbc[:], t["wdbcT"]).then_inc(fold_in, 16)
                sp.dma_start(par[:], t["par"]).then_inc(fold_in, 16)
                for n, name in enumerate(("g2", "b2", "bgate")):
                    sp.dma_start(cols[:, n, :], t[name]).then_inc(cols_in, 16)
                sp.dma_start(bfb[:], t["bf"].partition_broadcast(P)).then_inc(cols_in, 16)

            def gain_round_trip():
                sp.wait_ge(row_step, 4)
                sp.dma_start(scratch["gs"], rows[:, 4:6, :]).then_inc(gs_out, 16)
                sp.wait_ge(gs_out, 16)
                sp.dma_start(gs[:].rearrange("p b m d -> p (b m d)"),
                             scratch["gs"].rearrange("b m d -> (b m d)").partition_broadcast(P)).then_inc(gs_in, 16)

            def store_tokens(c):
                sp.wait_ge(xnt_ready, DT * (c + 1))
                for d in range(DT):
                    sp.dma_start(scratch["xn"][c, :, d, :].rearrange("p (j t) -> p j t", j=TB),
                                 xn_tile(c, d)).then_inc(xnt_out, 16)

            def store_folded(g):
                sp.wait_ge(wczt_ready, g + 1)
                sp.dma_start(scratch["wz"][g], wczt[:, g % 2, :]).then_inc(wcz_out[g % 2], 16)

            def store_projection(d, c):
                sp.wait_ge(dbo_ready[d], c + 1)
                sp.dma_start(scratch["dl"][d, c], dbo[0:R, d, :]).then_inc(dbo_out[d], 16)
                sp.dma_start(scratch["bc"][d, c], dbo[R:RD, d, :]).then_inc(dbo_out[d], 16)

            for f in range(NF):
                if f >= 2:
                    sp.wait_ge(bias_mm, f - 1)
                sp.dma_start(wct[:, f % 2], t["wcT"][f]).then_inc(wct_in[f % 2], 16)
                if f == 1:
                    load_small()
                if f in (1, 2):
                    half = slice((f - 1) * KE // 2, f * KE // 2)
                    sp.dma_start(wada[:, half, :], t["wadaT"][:, half, :]).then_inc(wada_in, 16)
                if f == FA + 1:
                    gain_round_trip()
                if f >= FX + 1:
                    store_tokens(f - FX - 1)
                    store_projection(0, f - FX - 1)
                if f >= 3:
                    store_folded(f - 3)
            store_folded(NF - 3)
            for c in range(NF - FX - 1, NC):
                store_tokens(c)
                store_projection(0, c)
            for g in range(NF - 2, NF):
                store_folded(g)
            sp.wait_ge(par_ready, 2)
            sp.wait_ge(bcz_ready, NF)
            sp.dma_start(scratch["par"].rearrange("f p n -> p f n"),
                         par[:].rearrange("p a e n -> p (a e) n")).then_inc(par_out, 16)
            for c in range(NC):
                store_projection(1, c)
            sp.wait_ge(par_out, 16)
            for j in range(2):
                sp.wait_ge(wcz_out[j], 16 * NF // 2)
                sp.wait_ge(dbo_out[j], 32 * NC)
            sp.wait_ge(xnt_out, 16 * DT * NC)

        @block.gpsimd
        def _(pool):
            nc.gpsimd.memset(mhalf[:], -0.5)
            nc.gpsimd.memset(t["zero"][:], 0.0)
            nc.gpsimd.memset(ident[:], 0.0).then_inc(id_ready, 1)
            pool.wait_ge(id_ready, 1)
            nc.gpsimd.affine_select(out=ident[:], in_=ident[:], compare_op=ALU.not_equal, fill=1.0, base=0,
                                    pattern=[[-1, P]], channel_multiplier=1).then_inc(id_ready, 1)
            pool.wait_ge(wada_in, 32)
            for k in range(2):
                pool.dma_start(xin[:, k], t["x"][k]).then_inc(x_in[k], 16)
            pool.wait_ge(gs_in, 16)
            pool.wait_ge(cols_in, 64)
            with pool.Fori(0, NC // 2) as b:
                for k in range(2):
                    c = 2 * b + k
                    for half in range(2):
                        pool.wait_ge(ve_ready, 2 * c + half + 1)
                        nc.gpsimd.tensor_tensor(rs[:], ve[:], mhalf[:], ALU.pow).then_inc(rs_ready, 1)
                    pool.wait_ge(x1_ready, TB * c + TB)
                    if k == 1:
                        pool.wait_ge(xsk_out, 16 * c)
                    for j in range(TB):
                        last = nc.gpsimd.tensor_tensor(xsk[:, j, :], xin[:, k, j, :], bfb[:], ALU.add)
                    last.then_inc(xsk_ready, 1)
                    pool.wait_ge(xsk_ready, c + 1)
                    pool.dma_start(scratch["xs"][c], xsk[:]).then_inc(xsk_out, 16)
                    pool.wait_ge(n2_ready, TB * (c + 1))
                    pool.dma_start(xin[:, k], t["x"][c + 2]).then_inc(x_in[k], 16)
                pool.wait_ge(xsk_out, 16 * c + 16)
            for k in range(2):
                pool.wait_ge(x_in[k], 16 * (NC // 2 + 1))
            pool.wait_ge(xsk_out, 16 * NC)

        @block.scalar
        def _(act):
            act.dma_start(wz[:], t["Wz"]).then_inc(wz_in, 16)
            nc.scalar.preload_act_table_set("natural_log_exp_and_others")
            act.wait_ge(cc_step, 1)
            nc.scalar.activation(cc[:], cc[:], ACT.Exp, scale=-1.0).then_inc(cc_step, 1)
            act.wait_ge(cc_step, 2)
            nc.scalar.activation(cc[:], cc[:], ACT.Ln, bias=1.0).then_inc(cc_step, 1)
            act.wait_ge(cc_step, 3)
            nc.scalar.activation(cc[:], cc[:], ACT.Exp, scale=-1.0).then_inc(cc_step, 1)
            act.wait_ge(fold_in, 48)
            nc.scalar.activation(par[:, :, :, PA:PA + N].rearrange("p a e n -> p (a e) n"),
                                 par[:, :, :, PA:PA + N].rearrange("p a e n -> p (a e) n"),
                                 ACT.Exp).then_inc(par_ready, 1)
            act.wait_ge(cols_in, 64)

            def transposed_tokens(c):
                for d in range(DT):
                    act.wait_ge(xnt_mm, DT * c + d + 1)
                    nc.scalar.activation(xn_tile(c, d), ps[7][:].rearrange("p (j t) -> p j t", j=TB), ACT.Identity,
                                         scale=cols[:, 0, d:d + 1], bias=cols[:, 1, d:d + 1]).then_inc(xnt_ready, 1)

            for f in range(NF + 1):
                if f >= FX:
                    transposed_tokens(f - FX)
                if f < NF:
                    act.wait_ge(fold_mm, f + 1)
                    if f >= 2:
                        act.wait_ge(wczt_mm, f - 1)
                    nc.scalar.activation(wcz[:, f % 2, :], ps[f % 2][:], ACT.Copy).then_inc(wcz_ready, 1)
                    act.wait_ge(bias_mm, f + 1)
                    bcz = par[:, f // ET, f % ET, PBZ:PBZ + 1]
                    nc.scalar.activation(bcz, ps[4][:, f:f + 1], ACT.Identity, bias=bcz).then_inc(bcz_ready, 1)
                if f >= 1:
                    act.wait_ge(wczt_mm, f)
                    if f >= 3:
                        act.wait_ge(wcz_out[(f - 1) % 2], 16 * ((f - 1) // 2))
                    nc.scalar.activation(wczt[:, (f - 1) % 2, :], ps[2 + (f - 1) % 2][:], ACT.Copy).then_inc(wczt_ready, 1)
                if f == ET:
                    nc.scalar.activation(wproj[:, 0].rearrange("p a r -> p (a r)"), ps[5][:, 0:DT * RD],
                                         ACT.Copy).then_inc(proj_ready[0], 1)
                    nc.scalar.activation(dbias[:, 0:1], ps[5][0:RD, DT * RD:DT * RD + 1],
                                         ACT.Copy).then_inc(proj_ready[0], 1)
                    act.wait_ge(proj_ready[0], 2)
                if f >= FX:
                    c = f - FX
                    act.wait_ge(dbc_mm[0], c + 1)
                    if c >= 1:
                        act.wait_ge(dbo_out[0], 32 * c)
                    nc.scalar.activation(dbo[:, 0, :], ps[5][0:RD, :], ACT.Identity,
                                         bias=dbias[:, 0:1]).then_inc(dbo_ready[0], 1)

        @block.vector
        def _(dve):
            dve.wait_ge(c_in, 16)
            nc.vector.tensor_scalar(cc[:], ct[:], LOW, None, ALU.max).then_inc(cc_step, 1)
            dve.wait_ge(cc_step, 4)
            nc.vector.tensor_tensor(ct[:], ct[:], cc[:], ALU.mult).then_inc(silu_ready, 1)
            dve.wait_ge(par_ready, 1)
            nc.vector.tensor_scalar(par[:, :, :, PA:PA + N].rearrange("p a e n -> p (a e) n"),
                                    par[:, :, :, PA:PA + N].rearrange("p a e n -> p (a e) n"),
                                    -1.0, None, ALU.mult).then_inc(par_ready, 1)
            dve.wait_ge(ada_mm, 2)
            dve.wait_ge(rows_in, 64)
            nc.vector.scalar_tensor_tensor(out=rows[:, 3, :], in0=ps[7][0:B, :], scalar=1.0, in1=rows[:, 3, :],
                                           op0=ALU.add, op1=ALU.add).then_inc(row_step, 1)
            nc.vector.tensor_tensor(rows[:, 2, :], ps[6][0:B, :], rows[:, 2, :], ALU.add).then_inc(row_step, 1)
            dve.wait_ge(row_step, 2)
            nc.vector.tensor_tensor(rows[:, 4, :], rows[:, 0, :], rows[:, 3, :], ALU.mult)
            nc.vector.tensor_tensor(rows[:, 1, :], rows[:, 1, :], rows[:, 3, :], ALU.mult).then_inc(row_step, 1)
            dve.wait_ge(row_step, 3)
            nc.vector.tensor_tensor(rows[:, 5, :], rows[:, 1, :], rows[:, 2, :], ALU.add).then_inc(row_step, 1)
            dve.wait_ge(cols_in, 64)
            dve.wait_ge(ada_mm, 3)
            for d in range(DT):
                nc.vector.tensor_scalar(gate[:, :, d], ps[4][:, NF + d * B:NF + (d + 1) * B], cols[:, 2, d:d + 1], None,
                                        ALU.add).then_inc(gate_ready, 1)
            dve.wait_ge(gs_in, 16)

            def normalise(c, b, k):
                for half in range(2):
                    for j in range(TB):
                        if half == 0 and j == 0:
                            dve.wait_ge(x_in[k], 16 * (b + 1))
                        if half == 1:
                            dve.wait_ge(x1_ready, TB * c + j + 1)
                        nc.vector.bn_stats(st[:, j, :], xin[:, k, j, :]).then_inc(stats_step, 1)
                    dve.wait_ge(stats_step, 16 * c + 8 * half + TB)
                    nc.vector.memset(pad[:], 0.0)
                    for j in range(TB):
                        nc.vector.bn_aggr(mv[:, j, :], st[:, j, :]).then_inc(stats_step, 1)
                    dve.wait_ge(stats_step, 16 * c + 8 * half + 8)
                    nc.vector.tensor_scalar(ve[:], mv[:, :, 1], EPS, None, ALU.add).then_inc(ve_ready, 1)
                    if half == 0:
                        for j in range(TB):
                            nc.vector.scalar_tensor_tensor(out=xin[:, k, j, :], in0=xin[:, k, j, :], scalar=mv[:, j, 0:1],
                                                           in1=gain[:], op0=ALU.subtract, op1=ALU.mult).then_inc(n1_ready, 1)
                        dve.wait_ge(rs_ready, 2 * c + 1)
                        for j in range(TB):
                            dve.wait_ge(n1_ready, TB * c + j + 1)
                            nc.vector.scalar_tensor_tensor(out=xin[:, k, j, :], in0=xin[:, k, j, :], scalar=rs[:, j:j + 1],
                                                           in1=shift[:], op0=ALU.mult, op1=ALU.add).then_inc(x1_ready, 1)
                    else:
                        dve.wait_ge(rs_ready, 2 * c + 2)
                        for j in range(TB):
                            nc.vector.tensor_scalar(xn2[:, bass.ds(TB * c + j, 1), :], xin[:, k, j, :], mv[:, j, 0:1],
                                                    rs[:, j:j + 1], ALU.subtract, ALU.mult).then_inc(n2_ready, 1)

            with dve.Fori(0, NC // 2) as b:
                nc.vector.tensor_copy(gain[:], gs[:, bass.ds(b, 1), 0, :])
                nc.vector.tensor_copy(shift[:], gs[:, bass.ds(b, 1), 1, :]).then_inc(gain_ready, 1)
                dve.wait_ge(gain_ready, b + 1)
                for k in range(2):
                    normalise(2 * b + k, b, k)
            dve.wait_ge(wczt_mm, NF)
            nc.vector.tensor_copy(wproj[:, 1].rearrange("p a r -> p (a r)"), ps[6][:, 0:DT * RD]).then_inc(proj_ready[1], 1)
            nc.vector.tensor_copy(dbias[:, 1:2], ps[6][0:RD, DT * RD:DT * RD + 1]).then_inc(proj_ready[1], 1)
            dve.wait_ge(proj_ready[1], 2)
            for c in range(NC):
                dve.wait_ge(dbc_mm[1], c + 1)
                if c >= 1:
                    dve.wait_ge(dbo_out[1], 32 * c)
                nc.vector.tensor_scalar(dbo[:, 1, :], ps[c % 2][0:RD, :], dbias[:, 1:2], None,
                                        ALU.add).then_inc(dbo_ready[1], 1)

        @block.tensor
        def _(pe):
            def modulate():
                pe.wait_ge(silu_ready, 1)
                pe.wait_ge(wada_in, 32)
                for m in range(2):
                    for k in range(KE):
                        last = nc.tensor.matmul(ps[6 + m][0:B, :], ct[:, k * B:(k + 1) * B], wada[:, k, m * D:(m + 1) * D],
                                                start=(k == 0), stop=(k == KE - 1))
                    last.then_inc(ada_mm, 1)
                pe.wait_ge(bcz_ready, FA)
                for d in range(DT):
                    for k in range(KE):
                        last = nc.tensor.matmul(ps[4][:, NF + d * B:NF + (d + 1) * B],
                                                wada[:, k, 2 * D + d * P:2 * D + (d + 1) * P],
                                                ct[:, k * B:(k + 1) * B], start=(k == 0), stop=(k == KE - 1),
                                                skip_group_check=True)
                last.then_inc(ada_mm, 1)

            def transposed(f):
                d, e = f // ET, f % ET
                pe.wait_ge(wcz_ready, f + 1)
                if f >= 2:
                    pe.wait_ge(wczt_ready, f - 1)
                for k in range(DT):
                    last = nc.tensor.matmul(ps[2 + f % 2][:, k * P:(k + 1) * P], wcz[:, f % 2, k * P:(k + 1) * P],
                                            ident[:], start=True, stop=True, is_transpose=True)
                for k in range(DT):
                    nc.tensor.matmul(ps[5 + d][:, k * RD:(k + 1) * RD], wcz[:, f % 2, k * P:(k + 1) * P],
                                     wdbc[:, d, e, :], start=(e == 0 and k == 0), stop=(e == ET - 1),
                                     skip_group_check=True)
                pe.wait_ge(bcz_ready, f + 1)
                last = nc.tensor.matmul(ps[5 + d][0:RD, DT * RD:DT * RD + 1], wdbc[:, d, e, :],
                                        par[:, d, e, PBZ:PBZ + 1], start=False, stop=(e == ET - 1),
                                        skip_group_check=True)
                last.then_inc(wczt_mm, 1)

            def transpose_tokens(c, d):
                pe.wait_ge(n2_ready, TB * (c + 1))
                if c + d > 0:
                    pe.wait_ge(xnt_ready, DT * c + d)
                for j in range(TB):
                    last = nc.tensor.matmul(ps[7][:, j * P:(j + 1) * P], xn2[:, TB * c + j, d * P:(d + 1) * P],
                                            ident[:], start=True, stop=True, is_transpose=True)
                last.then_inc(xnt_mm, 1)

            def project(d, c, bank):
                for k in range(DT):
                    last = nc.tensor.matmul(bank[0:RD, :], wproj[:, d, k, :], xn_tile(c, k),
                                            start=(k == 0), stop=(k == DT - 1))
                last.then_inc(dbc_mm[d], 1)

            pe.wait_ge(wz_in, 16)
            pe.wait_ge(id_ready, 2)
            for f in range(NF + 1):
                if f == FA:
                    modulate()
                if f < NF:
                    pe.wait_ge(wct_in[f % 2], 16 * (f // 2 + 1))
                    if f >= 2:
                        pe.wait_ge(wcz_ready, f - 1)
                for k in range(KE):
                    if f < NF:
                        last = nc.tensor.matmul(ps[f % 2][:], wct[:, f % 2, k, :], wz[:, k, :],
                                                start=(k == 0), stop=(k == KE - 1))
                        if k == KE - 1:
                            last.then_inc(fold_mm, 1)
                    if f >= FX and k % 2 == 1:
                        transpose_tokens(f - FX, k // 2)
                if f >= 1:
                    transposed(f - 1)
                if f == FA:
                    pe.wait_ge(gate_ready, DT)
                    pe.wait_ge(row_step, 2)
                if f == 0:
                    pe.wait_ge(fold_in, 48)
                if f < NF:
                    for k in range(KE):
                        last = nc.tensor.matmul(ps[4][:, f:f + 1], wct[:, f % 2, k, :], bz[:, k:k + 1],
                                                start=(k == 0), stop=(k == KE - 1), skip_group_check=True)
                    last.then_inc(bias_mm, 1)
                if f >= FX:
                    c = f - FX
                    pe.wait_ge(proj_ready[0], 2)
                    pe.wait_ge(xnt_ready, DT * (c + 1))
                    if c >= 1:
                        pe.wait_ge(dbo_ready[0], c)
                    project(0, c, ps[5])
            pe.wait_ge(wcz_ready, NF)
            pe.wait_ge(proj_ready[1], 2)
            for c in range(NC):
                if c >= 2:
                    pe.wait_ge(dbo_ready[1], c - 1)
                project(1, c, ps[c % 2])


def ssm_kernel(nc, t, scratch):
    with ExitStack() as ctx:
        def sb(name, shape):
            return ctx.enter_context(nc.sbuf_tensor(name, shape, fp32))

        def sem(name):
            return ctx.enter_context(nc.semaphore(name))

        gate, ident, zero = t["gate"], t["ident"], t["zero"]
        bcb = sb("bcb", [P, 2, GR, NG, TC])
        decay = sb("decay", [P, 2, NG, TC])
        state = sb("state", [P, GR, NG, TC])
        xn = sb("xn", [P, 2, DT, TC])
        dl = sb("dl", [R, 2, TC])
        wzs = sb("wzs", [P, 2, D])
        wdt = sb("wdt", [R, 2, P])
        wtail = sb("wtail", [P, 2, D])
        par = sb("upar", [P, 2, NP_])
        u, delta, du, ud = (sb(n, [P, 2, TC]) for n in ("u", "delta", "du", "ud"))
        soft = sb("soft", [P, TC])
        mx, sig = (sb(n, [P, TC]) for n in ("mx", "sig"))
        ym = sb("ym", [P, 2, 2, TC])
        yb = sb("yb", [P, TC])
        ygate = sb("ygate", [P, 2, TC])
        xskip = sb("xskip", [P, TB, D])
        res = sb("res", [P, DT, TC])
        carry = sb("carry", [P, ET * N])
        edge_decay = sb("edge_decay", [P, 2, N])
        inflow = sb("inflow", [P, 2, N])
        yps = [ctx.enter_context(nc.psum_tensor(f"yps{j}", [P, TC], fp32)) for j in range(2)]
        zps = ctx.enter_context(nc.psum_tensor("zps", [P, TC], fp32))
        dps = ctx.enter_context(nc.psum_tensor("dps", [P, TC], fp32))
        ops = [ctx.enter_context(nc.psum_tensor(f"ops{d}", [P, TC], fp32)) for d in range(DT)]

        unit_in, tail_in, xn_in, ym_in, ym_out = ([sem(f"{n}{j}") for j in range(2)] for n in (
            "unit_in", "tail_in", "xn_in", "ym_in", "ym_out"))
        b_in = [sem(f"b_in{g}") for g in range(GR)]
        c_in = [sem(f"c_in{g}") for g in range(GR)]
        xskip_in, res_in, res_out = sem("xskip_in"), sem("res_in"), sem("res_out")
        z_mm, d_mm, group_done, tr_mm, tail_mm, init_mm = (sem(n) for n in (
            "z_mm", "d_mm", "group_done", "tr_mm", "tail_mm", "init_mm"))
        u_ready, d_read, soft_step, soft_ready, ud_ready, decay_ready, mx_ready, sig_step, sig_ready = (
            sem(n) for n in ("u_ready", "d_read", "soft_step", "soft_ready", "ud_ready", "decay_ready",
                             "mx_ready", "sig_step", "sig_ready"))
        delta_ready, du_ready, scanned, prod_ready, y_read, clamp_ready, act_ready, y_ready, res_ready = (
            sem(n) for n in ("delta_ready", "du_ready", "scanned", "prod_ready", "y_read",
                             "clamp_ready", "act_ready", "y_ready", "res_ready"))
        carried, saved, dbu_ready, edge_ready, joined = (sem(n) for n in (
            "carried", "saved", "dbu_ready", "edge_ready", "joined"))
        block = ctx.enter_context(nc.Block())

        def done(count):
            return value(count + 1)

        class Unit:
            def __init__(self, b, db, s, i, n, final=False):
                def count(per_b, per_i, c):
                    return Count(b, i, per_b, per_i if n in (1, 2) else 0, c + db * per_b)

                self.b, self.s = count(1, 0, 0), s
                self.first, self.last = n == 0, n == ET - 1
                self.j = n % 2
                self.backward = s >= 2
                tile = count(0, 2, n)
                pair = count(0, 1, n // 2)
                self.tile = tile
                self.q = tile + count(UPB, 0, s * ET)
                self.qs = pair + count(UPB // 2, 0, s * (ET // 2))
                self.f = tile + count(2 * ET, 0, s * ET) if s < 2 else count(2 * ET, 0, 2 * ET)
                self.v = tile + count(2 * ET, 0, (s - 2) * ET) if s >= 2 else count(2 * ET, 0, 0)
                self.w = count(2, 0, max(s - 2, 0))
                self.direction = count(2, 0, s // 2)
                self.second = s % 2 == 1
                self.halves = self.direction * ET + tile
                self.start, self.end = (TC - 1, 0) if s >= 2 else (0, TC - 1)
                self.has_next_segment = not (final and s == SEGS - 1)
                self.has_next = self.has_next_segment or not self.last
                self.next_tile = count(0, 0, 0) if self.last else tile + 1
                self.next_s = (s + 1) % SEGS if self.last else s
                self.next_qs = self.qs + self.j
                self.has_prev = not (self.first and s == 0 and db == 0)
                self.prev_s = (s - 1) % SEGS if self.first else s
                self.prev_b = self.b - 1 if self.first and s == 0 else self.b
                self.prev_forward = self.has_prev and self.prev_s < 2
                self.prev_backward = self.has_prev and self.prev_s >= 2
                self.prev_tile = count(0, 0, ET - 1) if self.first else tile - 1
                self.prev_qs = self.qs - (1 - self.j)

        def units(eng, unit):
            def rest(b, final):
                for s in range(SEGS):
                    if s > 0:
                        unit(Unit(b, 0, s, None, 0, final))
                    with eng.Fori(0, (ET - 2) // 2) as i:
                        unit(Unit(b, 0, s, i, 1, final))
                        unit(Unit(b, 0, s, i, 2, final))
                    unit(Unit(b, 0, s, None, ET - 1, final))

            unit(Unit(0, 0, 0, None, 0))
            with eng.Fori(0, B - 1) as b:
                rest(b, False)
                unit(Unit(b, 1, 0, None, 0))
            rest(B - 1, True)
            return Unit(B - 1, 0, SEGS - 1, None, ET - 1, True)


        @block.sync
        def _(sp):
            for s in (res_out, *ym_out):
                sp.sem_inc(s, 16)

            def row(count):
                v = value(count)
                return v if isinstance(v, int) else sp.snap(v)

            def load_weights(j, tile):
                sp.dma_start(wzs[:, j, :], scratch["wz"][tile]).then_inc(unit_in[j], 16)
                sp.dma_start(wdt[:, j, :], t["wdtT"][tile]).then_inc(unit_in[j], 16)

            def load_parameters(j, tile):
                sp.dma_start(par[:, j, :], scratch["par"][tile]).then_inc(unit_in[j], 16)

            def load_tokens(chunk, s):
                sp.dma_start(xn[:, s % 2], scratch["xn"][chunk]).then_inc(xn_in[s % 2], 16)
                sp.dma_start(dl[:, s % 2, :], scratch["dl"][s // 2, chunk]).then_inc(xn_in[s % 2], 16)

            def load_row_group(which, chunk, s, g):
                rows = scratch["bc"][s // 2, chunk, N * which + NG * g:N * which + NG * (g + 1), :]
                sp.dma_start(bcb[:, which, g].rearrange("p n t -> p (n t)"),
                             rows.rearrange("n t -> (n t)").partition_broadcast(P)
                             ).then_inc((b_in, c_in)[which][g], 16)

            load_weights(0, 0)
            load_parameters(0, 0)
            load_tokens(0, 0)
            for g in range(GR):
                for which in range(2):
                    load_row_group(which, 0, 0, g)

            def reload_rows(which, g, q, chunk, s):
                sp.wait_ge((dbu_ready, prod_ready)[which], value(GR * q + g + 1))
                load_row_group(which, chunk, s, g)

            def unit(x):
                next_row, tile = row(x.next_tile + (x.next_s // 2) * ET), row(x.tile)
                chunk = row(x.b * 2 + HALF[x.s])
                nxt = row(x.b * 2 + (HALF[x.s + 1] if x.s < SEGS - 1 else 2))
                if x.has_prev:
                    before, prev_tile = row(x.prev_b * 2 + HALF[x.prev_s]), row(x.prev_tile)
                    mx_done, tails = row(x.f + 1), row(x.q)
                if x.has_next:
                    sp.wait_ge(decay_ready, done(GR * x.q))
                    load_weights(1 - x.j, next_row)
                    if x.prev_forward:
                        sp.wait_ge(mx_ready, mx_done)
                    load_parameters(1 - x.j, next_row)
                if x.has_prev:
                    sp.wait_ge(tail_mm, tails)
                sp.dma_start(wtail[:, x.j, :], t["wfT" if x.backward else "wxT"][tile]).then_inc(tail_in[x.j], 16)
                if x.first:
                    if x.has_prev:
                        for g in (1, 2, 3):
                            reload_rows(1, g, x.q - 1, chunk, x.s)
                    if x.has_next_segment:
                        sp.wait_ge(z_mm, value(x.q + 2))
                        load_tokens(nxt, (x.s + 1) % SEGS)
                    if x.backward:
                        sp.wait_ge(init_mm, done(x.w))
                        sp.dma_start(xskip[:], scratch["xs"][chunk]).then_inc(xskip_in, 16)
                if x.last and x.s == 3:
                    store_result(row(x.b * 2 + HALF[2]), x.w)
                if x.last and x.has_next_segment:
                    for which, g in ((0, 0), (0, 1), (0, 2), (0, 3), (1, 0)):
                        reload_rows(which, g, x.q, nxt, (x.s + 1) % SEGS)
                if x.prev_forward:
                    sp.wait_ge(act_ready, mx_done)
                    sp.dma_start(scratch["ym"][HALF[x.prev_s], prev_tile],
                                 ym[:, 1 - x.j]).then_inc(ym_out[1 - x.j], 16)
                if x.backward:
                    if x.s == 2:
                        sp.wait_ge(ym_out[x.j], value(16 * (x.b * ET + ET + 1)))
                    sp.dma_start(ym[:, x.j], scratch["ym"][HALF[x.s], tile]).then_inc(ym_in[x.j], 16)
                if x.first and x.s == 0 and x.has_prev:
                    store_result(before, x.w)
                if x.last and x.backward:
                    sp.wait_ge(res_out, value(16 * (x.w + 1)))
                    sp.dma_start(res[:], t["xT"][chunk]).then_inc(res_in, 16)

            def store_result(chunk, segments):
                sp.wait_ge(res_ready, done(DT * segments))
                sp.dma_start(t["out"][chunk], res[:]).then_inc(res_out, 16)

            x = units(sp, unit)
            store_result(2 * (B - 1) + HALF[x.s], x.w + 1)
            sp.wait_ge(res_out, 16 * (2 * B + 1))
            for j in range(2):
                sp.wait_ge(ym_out[j], 16 * (ET * B + 1))

        @block.tensor
        def _(pe):
            pe.sem_inc(group_done, GR)
            for s in (tail_mm, init_mm, tr_mm):
                pe.sem_inc(s, 1)

            def delta_product(j, s, q, qs, b_seg):
                pe.wait_ge(unit_in[j], value(48 * (qs + 1)))
                pe.wait_ge(xn_in[s % 2], value(32 * (b_seg + 1)))
                pe.wait_ge(d_read, done(q))
                nc.tensor.matmul(dps[:], wdt[:, j, :], dl[:, s % 2, :], start=True, stop=True).then_inc(d_mm, 1)

            def z_product(j, s):
                for k in range(DT):
                    last = nc.tensor.matmul(zps[:], wzs[:, j, k * P:(k + 1) * P], xn[:, s % 2, k, :],
                                            start=(k == 0), stop=(k == DT - 1))
                last.then_inc(z_mm, 1)

            def transpose_y(j, q, qs, b):
                pe.wait_ge(y_read, value(q + 3))
                pe.wait_ge(ym_in[j], value(16 * (qs - b * ET - ET + 1)))
                for k in range(TB):
                    nc.tensor.matmul(zps[:, k * P:(k + 1) * P], yb[:, k * P:(k + 1) * P], ident[:],
                                     start=(k == 0), stop=False, is_transpose=True, skip_group_check=True)
                for k in range(TB):
                    last = nc.tensor.matmul(zps[:, k * P:(k + 1) * P], ym[:, j, 0, k * P:(k + 1) * P], ident[:],
                                            start=False, stop=(k == TB - 1), is_transpose=True, skip_group_check=True)
                last.then_inc(tr_mm, 1)

            def project(j, v, qs, stop):
                pe.wait_ge(tail_in[j], value(16 * (qs + 1)))
                pe.wait_ge(y_ready, done(v + 1))
                for d in range(DT):
                    last = nc.tensor.matmul(ops[d][:], wtail[:, j, d * P:(d + 1) * P], ygate[:, j, :],
                                            start=False, stop=stop, skip_group_check=True)
                last.then_inc(tail_mm, 1)

            def transpose_group(j, q, g):
                pe.wait_ge(prod_ready, value(GR * q + g + 1))
                for n in range(NG):
                    for k in range(TB):
                        last = nc.tensor.matmul(yps[j][:, k * P:(k + 1) * P], state[:, g, n, k * P:(k + 1) * P],
                                                ident[:], start=False, stop=(g == GR - 1 and n == NG - 1),
                                                is_transpose=True, skip_group_check=True)
                last.then_inc(group_done, 1)

            def unit(x):
                if x.has_next:
                    pairs = x.b * 2 + (x.s // 2) if not x.last else x.b * 2 + ((x.s + 1) // 2)
                    delta_product(1 - x.j, x.next_s, x.q + 1, x.next_qs, pairs)
                if x.has_prev:
                    transpose_group(1 - x.j, x.q - 1, GR - 1)
                if x.has_next:
                    pe.wait_ge(u_ready, done(x.q + 1))
                    if x.prev_forward:
                        pe.wait_ge(mx_ready, done(x.f))
                    if x.prev_backward:
                        pe.wait_ge(y_ready, done(x.v - 1))
                    z_product(1 - x.j, x.next_s)
                for g in range(GR):
                    if g == 0:
                        pe.wait_ge(ud_ready, value(x.q + 1))
                        pe.wait_ge(y_read, value(x.q + 1))
                        for k in range(TB):
                            nc.tensor.matmul(yps[x.j][:, k * P:(k + 1) * P], ud[:, x.j, k * P:(k + 1) * P], ident[:],
                                             start=(k == 0), stop=False, is_transpose=True, skip_group_check=True)
                    if g == 0 and x.has_next and (x.prev_backward or not x.backward):
                        pe.wait_ge(u_ready, done(x.q + 2))
                    if g == 0 and x.prev_backward:
                        transpose_y(1 - x.j, x.q - 1, x.prev_qs, x.prev_b)
                    if g < GR - 1 or not x.has_next:
                        transpose_group(x.j, x.q, g)
                    if g == 0 and x.prev_backward:
                        project(1 - x.j, x.v - 1, x.prev_qs, x.first)
                    if g == 0 and not x.backward:
                        pe.wait_ge(tail_in[x.j], value(16 * (x.qs + 1)))
                        for k in range(DT):
                            last = nc.tensor.matmul(zps[:], wtail[:, x.j, k * P:(k + 1) * P], xn[:, x.s % 2, k, :],
                                                    start=(k == 0), stop=(k == DT - 1))
                        last.then_inc(tail_mm, 1)
                if x.first and x.backward:
                    pe.wait_ge(res_ready, done(DT * x.w))
                    pe.wait_ge(xskip_in, value(16 * (x.w + 1)))
                    for d in range(DT):
                        for k in range(TB):
                            last = nc.tensor.matmul(ops[d][:, k * P:(k + 1) * P], xskip[:, k, d * P:(d + 1) * P],
                                                    ident[:], start=(k == 0), stop=False, is_transpose=True,
                                                    skip_group_check=True)
                    last.then_inc(init_mm, 1)

            delta_product(0, 0, 0, 0, 0)
            z_product(0, 0)
            x = units(pe, unit)
            transpose_y(x.j, x.q, x.qs, x.b)
            project(x.j, x.v, x.qs, True)

        @block.scalar
        def _(act):
            nc.scalar.preload_act_table_set("natural_log_exp_and_others")
            for s in (d_read, u_ready, decay_ready, mx_ready):
                act.sem_inc(s, 1)
            act.sem_inc(y_read, 2)

            def read_backward_y(j, q, v):
                act.wait_ge(group_done, value(GR * (q + 2)))
                act.wait_ge(tr_mm, done(v))
                nc.scalar.activation(yb[:], yps[j][:], ACT.Copy).then_inc(y_read, 1)

            def start_delta(j, q, qs):
                act.wait_ge(unit_in[j], value(48 * (qs + 1)))
                act.wait_ge(d_mm, value(q + 1))
                nc.scalar.activation(soft[:], dps[:], ACT.Abs, bias=par[:, j, PBD:PBD + 1]).then_inc(soft_step, 1)
                nc.scalar.activation(delta[:, j, :], dps[:], ACT.Relu, bias=par[:, j, PBD:PBD + 1]).then_inc(d_read, 1)
                act.wait_ge(soft_step, value(2 * q + 1))
                nc.scalar.activation(soft[:], soft[:], ACT.Exp, scale=-1.0).then_inc(soft_step, 1)
                act.wait_ge(soft_step, value(2 * q + 2))
                nc.scalar.activation(soft[:], soft[:], ACT.Ln, bias=1.0).then_inc(soft_ready, 1)

            def read_z(j, q):
                act.wait_ge(z_mm, value(q + 1))
                nc.scalar.activation(u[:, j, :], zps[:], ACT.Identity, bias=par[:, j, PBZ:PBZ + 1]).then_inc(u_ready, 1)
                act.wait_ge(u_ready, done(q + 1))
                if q != 0:
                    act.wait_ge(group_done, value(GR * q))
                nc.scalar.activation(ud[:, j, :], u[:, j, :], ACT.Copy, scale=par[:, j, PDP:PDP + 1]).then_inc(ud_ready, 1)

            def save_carry(x, g):
                act.wait_ge(scanned, value(GR * x.q + g + 3))
                nc.scalar.activation(carry[:, bass.ds(value(x.tile * N + NG * g), NG)],
                                     state[:, g, :, x.end], ACT.Copy).then_inc(saved, 1)

            def unit(x):
                tokens = slice(0, TC - 1) if x.backward else slice(1, TC)
                for g in range(GR):
                    if g == 0:
                        act.wait_ge(delta_ready, value(x.q + 1))
                    if g == 0 and x.second:
                        nc.scalar.activation(edge_decay[:, x.j, :], par[:, x.j, PA:PA + N], ACT.Exp,
                                             scale=delta[:, x.j, x.start:x.start + 1]).then_inc(edge_ready, 1)
                    if g >= 2 and not x.second:
                        if x.first and g == 2:
                            act.wait_ge(carried, done(ET * x.direction))
                        save_carry(x, g - 2)
                    act.wait_ge(scanned, value(GR * x.q + g + 1))
                    if x.first and not x.second and g < 2:
                        nc.scalar.activation(decay[:, g, :, x.start], zero[:], ACT.Copy)
                    for n in range(NG):
                        m = NG * g + n
                        last = nc.scalar.activation(decay[:, g % 2, n, tokens], delta[:, x.j, tokens], ACT.Exp,
                                                    scale=par[:, x.j, PA + m:PA + m + 1])
                    last.then_inc(decay_ready, 1)
                    if g == 1 and x.has_next:
                        act.wait_ge(decay_ready, done(GR * x.q))
                        start_delta(1 - x.j, x.q + 1, x.next_qs)
                    if g == 2 and x.prev_backward:
                        read_backward_y(1 - x.j, x.q - 1, x.v - 1)
                    if g == 2 and x.has_next:
                        read_z(1 - x.j, x.q + 1)
                    if g == 2 and x.prev_forward:
                        if x.prev_s == 0:
                            act.wait_ge(y_ready, done(2 * ET * x.b))
                        act.wait_ge(ym_out[1 - x.j], value(16 * (x.prev_qs - x.b * ET + 1)))
                        act.wait_ge(group_done, value(GR * (x.q + 1)))
                        nc.scalar.activation(ym[:, 1 - x.j, 0, :], yps[1 - x.j][:], ACT.Copy).then_inc(y_read, 1)
                    if g == 3 and x.prev_forward:
                        act.wait_ge(clamp_ready, value(x.f))
                        nc.scalar.activation(sig[:], sig[:], ACT.Exp, scale=-1.0).then_inc(sig_step, 1)
                        act.wait_ge(sig_step, value(2 * x.f - 1))
                        nc.scalar.activation(sig[:], sig[:], ACT.Ln, bias=1.0).then_inc(sig_step, 1)
                        act.wait_ge(sig_step, value(2 * x.f))
                        nc.scalar.activation(sig[:], sig[:], ACT.Exp, scale=-1.0).then_inc(sig_ready, 1)
                if not x.second:
                    save_carry(x, 2)
                if not x.backward:
                    act.wait_ge(tail_mm, done(x.q + 1))
                    act.wait_ge(act_ready, done(x.f))
                    nc.scalar.activation(mx[:], zps[:], ACT.Identity, bias=par[:, x.j, PBX:PBX + 1]).then_inc(mx_ready, 1)
                if not x.second:
                    save_carry(x, 3)

            start_delta(0, 0, 0)
            read_z(0, 0)
            x = units(act, unit)
            read_backward_y(x.j, x.q, x.v)

        @block.gpsimd
        def _(pool):
            def unit(x):
                for g in range(GR):
                    if g == 0:
                        pool.wait_ge(delta_ready, value(x.q + 1))
                        pool.wait_ge(u_ready, done(x.q + 1))
                        nc.gpsimd.tensor_tensor(du[:, x.j, :], delta[:, x.j, :], u[:, x.j, :], ALU.mult).then_inc(du_ready, 1)
                        pool.wait_ge(du_ready, value(x.q + 1))
                    pool.wait_ge(b_in[g], value(16 * (x.b * SEGS + x.s + 1)))
                    pool.wait_ge(group_done, value(GR * x.q + g + 1))
                    nc.gpsimd.tensor_tensor(state[:, g], bcb[:, 0, g],
                                            du[:, x.j:x.j + 1, :].broadcast_to([P, NG, TC]),
                                            ALU.mult).then_inc(dbu_ready, 1)

            units(pool, unit)

        @block.vector
        def _(dve):
            dve.sem_inc(scanned, 2)
            for s in (act_ready, y_ready, res_ready, carried):
                dve.sem_inc(s, 1)

            def finish_delta(j, q):
                dve.wait_ge(soft_ready, value(q + 1))
                nc.vector.tensor_tensor(delta[:, j, :], delta[:, j, :], soft[:], ALU.add).then_inc(delta_ready, 1)

            def gate_y(j, v, tails):
                dve.wait_ge(tr_mm, done(v + 1))
                dve.wait_ge(tail_mm, done(tails))
                nc.vector.tensor_tensor(ygate[:, j, :], zps[:], ym[:, j, 1, :], ALU.mult).then_inc(y_ready, 1)

            def results(b, w, tails):
                dve.wait_ge(tail_mm, done(tails))
                dve.wait_ge(res_in, value(16 * (w + 1)))
                for d in range(DT):
                    nc.vector.scalar_tensor_tensor(out=res[:, d, :], in0=ops[d][:], scalar=gate[:, bass.ds(value(b), 1), d],
                                                   in1=res[:, d, :], op0=ALU.mult, op1=ALU.add).then_inc(res_ready, 1)

            def unit(x):
                step = -1 if x.backward else 1

                def product(g):
                    dve.wait_ge(c_in[g], value(16 * (x.b * SEGS + x.s + 1)))
                    dve.wait_ge(scanned, value(GR * x.q + g + 3))
                    if not x.second:
                        dve.wait_ge(saved, value(x.halves * GR + g + 1))
                    nc.vector.tensor_tensor(state[:, g], state[:, g], bcb[:, 1, g], ALU.mult).then_inc(prod_ready, 1)

                def join(g):
                    dve.wait_ge(dbu_ready, value(GR * x.q + g + 1))
                    if g == 0:
                        dve.wait_ge(carried, done(x.halves + 1))
                    nc.vector.tensor_tensor(state[:, g, :, x.start], state[:, g, :, x.start],
                                            inflow[:, x.j, NG * g:NG * (g + 1)], ALU.add).then_inc(joined, 1)

                for g in range(GR):
                    if x.second and g < 2:
                        join(g)
                    if x.second:
                        dve.wait_ge(joined, value(x.halves * GR + g + 1))
                    else:
                        dve.wait_ge(dbu_ready, value(GR * x.q + g + 1))
                    dve.wait_ge(decay_ready, done(GR * x.q + g + 1))
                    h = state[:, g].rearrange("p n t -> p (n t)")[:, ::step]
                    nc.vector.tensor_tensor_scan(h, decay[:, g % 2].rearrange("p n t -> p (n t)")[:, ::step], h, 0.0,
                                                 ALU.mult, ALU.add).then_inc(scanned, 1)
                    if g == 0 and x.prev_forward:
                        dve.wait_ge(mx_ready, done(x.f))
                        dve.wait_ge(act_ready, done(x.f - 1))
                        nc.vector.tensor_scalar(sig[:], mx[:], LOW, None, ALU.max).then_inc(clamp_ready, 1)
                    if g == 2 and x.prev_backward:
                        gate_y(1 - x.j, x.v - 1, x.q - 2)
                    if g == 3 and x.prev_forward:
                        if x.prev_s == 0:
                            dve.wait_ge(y_ready, done(2 * ET * x.b))
                        dve.wait_ge(ym_out[1 - x.j], value(16 * (x.prev_qs - x.b * ET + 1)))
                        dve.wait_ge(sig_ready, value(x.f))
                        nc.vector.tensor_tensor(ym[:, 1 - x.j, 1, :], mx[:], sig[:], ALU.mult).then_inc(act_ready, 1)
                    if g == 3 and x.first and x.prev_backward:
                        results(x.prev_b, x.w - 1, x.q)
                    if x.second and g == 2:
                        join(3)
                    if g > 0:
                        product(g - 1)
                    if x.second and g == 1:
                        join(2)
                    if g == 1 and x.has_next:
                        finish_delta(1 - x.j, x.q + 1)
                if x.has_next and x.next_s % 2 == 1:
                    before = (x.b * 2 + x.next_s // 2) * ET + x.next_tile
                    dve.wait_ge(saved, value((before + 1) * GR))
                    dve.wait_ge(edge_ready, value(before + 1))
                    nc.vector.tensor_tensor(inflow[:, 1 - x.j, :], carry[:, bass.ds(value(x.next_tile * N), N)],
                                            edge_decay[:, 1 - x.j, :], ALU.mult).then_inc(carried, 1)
                product(GR - 1)

            finish_delta(0, 0)
            x = units(dve, unit)
            gate_y(x.j, x.v, x.q - 1)
            results(x.b, x.w, x.q + 1)


def build(nc, t):
    with ExitStack() as ctx:
        scratch = {
            "gs": nc.dram_tensor("gs_s", (B, 2, D), fp32).ap(),
            "wz": nc.dram_tensor("wz_s", (2 * ET, P, D), fp32).ap(),
            "par": nc.dram_tensor("par_s", (2 * ET, P, NP_), fp32).ap(),
            "xn": nc.dram_tensor("xn_s", (NC, P, DT, TC), fp32).ap(),
            "dl": nc.dram_tensor("dl_s", (2, NC, R, TC), fp32).ap(),
            "bc": nc.dram_tensor("bc_s", (2, NC, 2 * N, TC), fp32).ap(),
            "xs": nc.dram_tensor("xs_s", (NC, P, TB, D), fp32).ap(),
            "ym": nc.dram_tensor("ym_s", (2, ET, P, 2, TC), fp32).ap(),
        }
        t["gate"] = ctx.enter_context(nc.sbuf_tensor("gate", [P, B, DT], fp32))
        t["ident"] = ctx.enter_context(nc.sbuf_tensor("ident", [P, P], fp32))
        t["zero"] = ctx.enter_context(nc.sbuf_tensor("zero", [P, NG], fp32))
        setup_kernel(nc, t, scratch)
        ssm_kernel(nc, t, scratch)


def kernel(**inputs):
    import numpy as np
    import concourse.bacc as bacc
    from concourse.bass_utils import run_bass_kernel_spmd

    a = {k.replace("L0_cond_", ""): np.asarray(v) for k, v in inputs.items()}

    def tiles(m):
        return m.reshape(m.shape[0] // P, P, *m.shape[1:]).swapaxes(0, 1)

    x = a["x"]
    xc = x.reshape(NC, TB, P, D).transpose(0, 2, 1, 3)
    par = np.concatenate([np.concatenate([
        tiles(a[f"Alog{d}"]),
        *(tiles(a[n].reshape(E, 1)) for n in (f"bc{d}", f"bdt{d}", f"Dp{d}", "bx"))], axis=2)[:, None]
        for d in (1, 2)], axis=1)
    arrays = {
        "x": np.concatenate([xc, xc[:2]]),
        "xT": x.reshape(B, 2, TC, DT, P).transpose(0, 1, 4, 3, 2).reshape(NC, P, DT, TC),
        "cT": tiles(a["cond_2048"].T).reshape(P, KE * B),
        "wadaT": tiles(a["Wada"].T),
        "g1": a["norm1_g"], "b1": a["norm1_b"], "bada": a["bada"], "bf": a["bf"],
        "g2": a["norm2_g"].reshape(DT, P).T, "b2": a["norm2_b"].reshape(DT, P).T,
        "bgate": a["bada"][2 * D:].reshape(DT, P).T,
        "Wz": tiles(a["Wz"]), "bz": a["bz"].reshape(KE, P).T,
        "wcT": np.concatenate([a[f"Wc{d}"].reshape(ET, P, KE, P).transpose(0, 3, 2, 1) for d in (1, 2)]),
        "wdbcT": np.stack([tiles(a[f"Wdbc{d}"].T) for d in (1, 2)], axis=1),
        "wdtT": np.concatenate([a[f"Wdt{d}"].reshape(ET, P, R).transpose(0, 2, 1) for d in (1, 2)]),
        "wxT": a["Wx"].reshape(ET, P, DT, P).transpose(0, 3, 2, 1).reshape(ET, P, D),
        "wfT": a["Wf"].T.reshape(ET, P, D),
        "par": par,
    }
    nc = bacc.Bacc("TRN2", target_bir_lowering=False, num_devices=1)
    feed, t = {}, {}
    for name, v in arrays.items():
        v = np.ascontiguousarray(v)
        feed[f"in_{name}"] = v
        t[name] = nc.dram_tensor(f"in_{name}", v.shape, mybir.dt.from_np(v.dtype), kind="ExternalInput").ap()
    t["out"] = nc.dram_tensor("out_t", (NC, P, DT, TC), fp32, kind="ExternalOutput").ap()
    build(nc, t)
    got = run_bass_kernel_spmd(nc, [feed], core_ids=[0])
    return np.ascontiguousarray(got.results[0]["out_t"].transpose(0, 3, 2, 1).reshape(B, S, D))
```
